# Optimizing a Trainium2 kernel written in Bass

```python
import numpy as np
import jax
import jax.numpy as jnp

def _softmax(x, axis=-1):
    return jax.nn.softmax(x, axis=axis)
def _gelu(x):
    return jax.nn.gelu(x, approximate=True)
def _silu(x):
    return jax.nn.silu(x)
def _sigmoid(x):
    return jax.nn.sigmoid(x)
def _layernorm(x, axis=-1, eps=1e-5):
    m = jnp.mean(x, axis=axis, keepdims=True)
    v = jnp.var(x, axis=axis, keepdims=True)
    return (x - m) / jnp.sqrt(v + eps)
def _scatter_add(tgt, idx, src, axis=0):
    return tgt.at[idx].add(src)
def _segment_sum(src, seg, n):
    return jax.ops.segment_sum(src, seg, n)

kernel_name = 'mk_adj_preln_d1_adj_128_b05fe6'

def setup_inputs(seed: int = 0):
    np.random.seed(seed)
    _w = jnp.asarray
    def _rec_inputs():
        import jax
        import jax.numpy as jnp
        _gk = jax.random.key(seed)
        x = -0.000929 + 1 * jax.random.normal(jax.random.fold_in(_gk, 1), (8192, 128), jnp.float32)
        _a = jax.random.bernoulli(jax.random.fold_in(_gk, 2), 0.000488281, (8192, 8192))
        _a = jnp.logical_or(_a, jnp.swapaxes(_a, -1, -2))
        _a = jnp.logical_or(_a, jnp.eye(8192, dtype=bool))
        adj = _a.astype(jnp.int32)
        return x, adj
    x, adj = _rec_inputs()
    def _L0_gnn_setup():
        import jax, jax.numpy as jnp
        import numpy as np
        N = 8192
        IN_F = 128
        OUT_F = 128
        ALPHA = 0.2
        NEG_INF = -9000000000000000.0
        key = jax.random.key(seed)
        k1, k2, k3, k4 = jax.random.split(key, 4)
        h = jax.random.normal(k1, (N, IN_F), dtype=jnp.float32)
        adj = jax.random.randint(k2, (N, N), 0, 2, dtype=jnp.int32)
        W = jax.random.normal(k3, (IN_F, OUT_F), dtype=jnp.float32) * (1.0 / np.sqrt(IN_F))
        limit = 1.414 * np.sqrt(6.0 / (2 * OUT_F + 1))
        a = jax.random.uniform(k4, (2 * OUT_F, 1), dtype=jnp.float32, minval=-limit, maxval=limit)
        return {'h': h, 'adj': adj, 'W': W, 'a': a}
    _L0_gnn_all = _L0_gnn_setup()
    _L0_gnn_in = {k: v for k, v in _L0_gnn_all.items() if k in ('W', 'a', )}
    del _L0_gnn_all

    return {
        "x": x,
        "adj": adj,
        "L0_gnn_W": _L0_gnn_in["W"],
        "L0_gnn_a": _L0_gnn_in["a"],
    }

def reference(x, adj, L0_gnn_W, L0_gnn_a):
    import jax
    import jax.numpy as jnp
    def _L0_gnn_ref(h, adj, W, a):
        import jax, jax.numpy as jnp
        import numpy as np
        N = 8192
        IN_F = 128
        OUT_F = 128
        ALPHA = 0.2
        NEG_INF = -9000000000000000.0
        Wh = h @ W
        a1 = a[:OUT_F, 0]
        a2 = a[OUT_F:, 0]
        s1 = Wh @ a1
        s2 = Wh @ a2
        e = jax.nn.leaky_relu(s1[:, None] + s2[None, :], negative_slope=ALPHA)
        masked = jnp.where(adj > 0, e, NEG_INF)
        attention = jax.nn.softmax(masked, axis=1)
        h_prime = attention @ Wh
        return jax.nn.elu(h_prime)

    h = jnp.maximum(_layernorm(x, axis=-1), 0.0)
    x = x + _L0_gnn_ref(h, adj, L0_gnn_W, L0_gnn_a)
    return x


_drawn_inputs = setup_inputs


def setup_inputs(seed=0):
    import zlib

    import numpy as np

    out = dict(_drawn_inputs(seed))
    spreads = {}
    factors = {}
    for name, (base, spread) in spreads.items():
        noise = np.random.default_rng([zlib.crc32(name.encode()), seed]).standard_normal(out[name].shape)
        drawn = base * np.exp(spread * noise) if base else spread * noise
        out[name] = jnp.asarray(drawn.astype(out[name].dtype))
    for name, factor in factors.items():
        out[name] = (out[name] * factor).astype(out[name].dtype)
    return out
```

```python
from contextlib import ExitStack

import concourse.bass as bass
from concourse import mybir

ALU = mybir.AluOpType
ACT = mybir.ActivationFunctionType
AX_X = mybir.AxisListType.X
F32 = mybir.dt.float32
BF16 = mybir.dt.bfloat16
I32 = mybir.dt.int32

P = 128
SLOPE = 0.2
MASKED = -9000000000000000.0
LN_EPS = 1e-5
SAFE_SPREAD = 60.0
GATE_SCALE = 280.0
GATE_BIAS = -200.0

ROWS = 4
CHUNK = 1024
STEPS = CHUNK // P
RAW_SLOTS = 4
GATE_SLOTS = 2
WT_SLOTS = 4
LEAD = 3
GROUP = 4


def graph_attention(nc, x, adj, w, a, out):
    N, F = x.shape
    NT = N // P
    BANDS = N // (ROWS * P)
    BAND = ROWS * P
    CHUNKS = N // CHUNK
    GROUPS = NT // GROUP
    FD = F + 1
    PAIR = 2 * STEPS
    PAIRS = CHUNKS // 2
    BAND_STEPS = NT
    GATHER = 4
    assert F == P and CHUNKS % RAW_SLOTS == 0 and PAIR % WT_SLOTS == 0 and BANDS % 2 == 0

    with ExitStack() as ctx:
        def sb(name, shape, dt=F32):
            return ctx.enter_context(nc.sbuf_tensor(name, shape, dt))

        def sem(name):
            return ctx.enter_context(nc.semaphore(name))

        raw = sb("raw", [P, RAW_SLOTS, ROWS, CHUNK], I32)
        gate = sb("gate", [P, GATE_SLOTS, ROWS, CHUNK], BF16)
        xs = sb("xs", [P, NT, F])
        rbc = sb("rbc", [P, N])
        wh = sb("wh", [P, NT, FD])
        weights = sb("weights", [P, WT_SLOTS, BAND])
        hacc = sb("hacc", [P, 2, ROWS, FD])
        obuf = sb("obuf", [P, 2, ROWS, F])
        hp = sb("hp", [P, ROWS, F])
        neg = sb("neg", [P, ROWS, F])
        xn = weights[:, 0:2, :].rearrange("p s (t f) -> p s t f", f=F)
        ht = weights[:, 2:4, :]
        identf = sb("identf", [P, P])
        identb = sb("identb", [P, P], BF16)
        zeros = sb("zeros", [P, 2 * FD], BF16)
        wext = sb("wext", [P, FD])
        wt = sb("wt", [P, P])
        wa1 = sb("wa1", [P, P])
        a12 = sb("a12", [P, 2])
        a1bc = sb("a1bc", [P, P])
        stats = sb("stats", [P, NT, 6])
        mean = sb("mean", [P, NT])
        rstd = sb("rstd", [P, NT])
        tmp1 = sb("tmp1", [P, NT])
        tmp2 = sb("tmp2", [P, NT])
        hsum = sb("hsum", [P, GROUPS])
        htot = sb("htot", [P, 1])
        hmean = sb("hmean", [P, P])
        mean_wh = sb("mean_wh", [P, F])
        ext = sb("ext", [P, 2])
        gext = sb("gext", [P, 2])
        spread = sb("spread", [P, 1])
        flag = sb("flag", [P, 1], I32)
        bias = sb("bias", [P, 3])
        dcol = sb("dcol", [P, NT])
        beta = sb("beta", [P, NT])
        empty = sb("empty", [P, 2, ROWS])
        rden = sb("rden", [P, 2, ROWS])
        s1col = sb("s1col", [P, NT])
        nmax = sb("nmax", [P, 1])

        ps = ctx.enter_context(nc.psum_tensor("ps", [P, 8, 512], F32))
        acc = [ps[:, 2 * k:2 * k + 2, 0:2 * FD] for k in range(2)]
        turned = [ps[:, 4 + k, 0:BAND // 2].bitcast(BF16) for k in range(WT_SLOTS)]

        w_in, a_in = sem("w_in"), sem("a_in")
        x_in = [sem(f"x_in{k}") for k in range(4)]
        raw_in = [sem(f"raw_in{k}") for k in range(RAW_SLOTS)]
        out_done = [sem(f"out_done{k}") for k in range(2)]
        consts = sem("consts")
        dve_chain, pool_chain, stats_done = sem("dve_chain"), sem("pool_chain"), sem("stats_done")
        wt_turned, wt_ready, a1_ready, wa_done, wa_ready = (
            sem("wt_turned"), sem("wt_ready"), sem("a1_ready"), sem("wa_done"), sem("wa_ready"))
        var_ready, std_ready = sem("var_ready"), sem("std_ready")
        xn_ready, xt_ready, ht_ready = sem("xn_ready"), sem("xt_ready"), sem("ht_ready")
        wh_done, wh_copied = sem("wh_done"), sem("wh_copied")
        s1_done, s1_copied = sem("s1_done"), sem("s1_copied")
        hmean_ready, mwh_done, mwh_ready = sem("hmean_ready"), sem("mwh_done"), sem("mwh_ready")
        ext_ready, gext_ready, flag_ready = sem("ext_ready"), sem("gext_ready"), sem("flag_ready")
        d_ready, z_ready, r_ready, w_ready = sem("d_ready"), sem("z_ready"), sem("r_ready"), sem("w_ready")
        gate_ready = sem("gate_ready")
        turned_ready = sem("turned_ready")
        weights_ready = sem("weights_ready")
        weights_used = sem("weights_used")
        sums_copied = sem("sums_copied")
        hacc_free = sem("hacc_free")
        rden_ready, neg_ready, exp_ready, out_ready = (
            sem("rden_ready"), sem("neg_ready"), sem("exp_ready"), sem("out_ready"))
        g_diag, g_spread = sem("g_diag"), sem("g_spread")
        g_adj, g_adj_free = sem("g_adj"), sem("g_adj_free")
        g_scores, g_probs = sem("g_scores"), sem("g_probs")
        g_turned, g_copied, g_used = sem("g_turned"), sem("g_copied"), sem("g_used")

        scores = raw[:, 2:4, :, :].rearrange("p s t j -> p (s t j)").bitcast(F32)
        adj_rows = raw[:, 0:2, :, :].rearrange("p s t j -> p (s t j)")
        x_tiles = x.rearrange("(t p) f -> p t f", p=P)
        adj_tiles = adj.rearrange("(t p) j -> p t j", p=P)
        out_tiles = out.rearrange("(t p) f -> p t f", p=P)

        def safe(eng):
            eng.wait_ge(flag_ready, 1)
            return eng.value_load(flag[0:1, 0:1], min_val=0, max_val=1) == 1

        block = ctx.enter_context(nc.Block())

        @block.sync
        def _(sp):
            sp.dma_start(wext[:, 0:F], w).then_inc(w_in, 16)
            for k in range(2):
                sp.dma_start(a12[:, k:k + 1], a[k * F:(k + 1) * F, :]).then_inc(a_in, 16)
            for k in range(4):
                n = NT // 4
                sp.dma_start(xs[:, k * n:(k + 1) * n, :], x_tiles[:, k * n:(k + 1) * n, :]).then_inc(x_in[k], 16)

            def load(band, chunk, slot):
                rows = bass.ds(band * ROWS, ROWS)
                sp.dma_start(raw[:, slot, :, :], adj_tiles[:, rows, chunk * CHUNK:(chunk + 1) * CHUNK])\
                    .then_inc(raw_in[slot], 16)

            for k in range(RAW_SLOTS):
                load(0, k, k)

            def safe_path():
                for k in range(RAW_SLOTS, CHUNKS):
                    sp.wait_ge(gate_ready, k - RAW_SLOTS + 1)
                    load(0, k, k % RAW_SLOTS)
                with sp.Fori(1, BANDS) as band:
                    for k in range(CHUNKS):
                        sp.wait_ge(gate_ready, band * CHUNKS + (k - RAW_SLOTS + 1))
                        load(band, k, k % RAW_SLOTS)

            def general_path():
                for k in range(RAW_SLOTS):
                    sp.wait_ge(raw_in[k], 16)
                with sp.Fori(0, NT) as tile:
                    sp.wait_ge(g_adj_free, tile + 1)
                    sp.dma_start(adj_rows, adj_tiles[:, bass.ds(tile, 1), :].rearrange("p t j -> p (t j)"))\
                        .then_inc(g_adj, 16)

            with sp.If(safe(sp)):
                safe_path()
                sp.nop()
            with sp.Else():
                general_path()
                sp.nop()
            sp.nop()

        @block.gpsimd
        def _(pool):
            links = [0]

            def link(ins):
                links[0] += 1
                ins.then_inc(pool_chain, 1)
                pool.wait_ge(pool_chain, links[0])

            pool.sem_inc(hacc_free, 2)
            link(nc.gpsimd.memset(identf[:, :], 0.0))
            link(nc.gpsimd.affine_select(out=identf[:, :], in_=identf[:, :], compare_op=ALU.not_equal, fill=1.0,
                                         base=0, pattern=[[-1, P]], channel_multiplier=1))
            nc.gpsimd.tensor_copy(identb[:, :], identf[:, :]).then_inc(consts, 1)
            nc.gpsimd.memset(bias[:, 2:3], GATE_BIAS).then_inc(consts, 1)
            nc.gpsimd.memset(zeros[:, :], 0.0).then_inc(consts, 1)
            pool.wait_ge(ext_ready, 1)
            nc.gpsimd.partition_all_reduce(gext[:, :], ext[:, :], P, bass.bass_isa.ReduceOp.max)\
                .then_inc(gext_ready, 1)

            LINKS = 4
            base = links[0]

            def finish_band(band, half, tiles, first, stored=None):
                done = [0]

                def chained(ins):
                    done[0] += 1
                    ins.then_inc(pool_chain, 1)
                    pool.wait_ge(pool_chain, band * LINKS + (base + done[0]))

                h, n, o = hp[:, 0:tiles, :], neg[:, 0:tiles, :], obuf[:, half, 0:tiles, :]
                row = [P, tiles, F]
                pool.wait_ge(rden_ready, band + 1)
                nc.gpsimd.tensor_tensor(n, empty[:, half, 0:tiles].unsqueeze(2).to_broadcast(row),
                                        mean_wh[:, :].unsqueeze(1).to_broadcast(row), ALU.mult)
                chained(nc.gpsimd.tensor_tensor(h, hacc[:, half, 0:tiles, 0:F],
                                                rden[:, half, 0:tiles].unsqueeze(2).to_broadcast(row), ALU.mult))
                chained(nc.gpsimd.tensor_tensor(h, h, n, ALU.add))
                pool.sem_inc(hacc_free, 1)
                nc.gpsimd.tensor_scalar(n, h, 0.0, None, ALU.min).then_inc(neg_ready, 1)
                chained(nc.gpsimd.tensor_scalar(h, h, 0.0, -1.0, ALU.max, ALU.add))
                if stored is not None:
                    pool.wait_ge(out_done[half], stored * 16)
                chained(nc.gpsimd.tensor_tensor(o, h, xs[:, bass.ds(first, tiles), :], ALU.add))
                pool.wait_ge(exp_ready, band + 1)
                nc.gpsimd.tensor_tensor(o, o, n, ALU.add).then_inc(out_ready, 1)
                pool.wait_ge(out_ready, band + 1)
                pool.dma_start(out_tiles[:, bass.ds(first, tiles), :], o).then_inc(out_done[half], 16)

            def finish_all(bands, tiles):
                pool.wait_ge(mwh_ready, 1)
                finish_band(0, 0, tiles, 0)
                finish_band(1, 1, tiles, tiles)
                with pool.Fori(1, bands // 2) as pair:
                    for half in range(2):
                        finish_band(pair * 2 + half, half, tiles, pair * (2 * tiles) + half * tiles, stored=pair)
                for half in range(2):
                    pool.wait_ge(out_done[half], 16 * (bands // 2))

            def safe_path():
                pool.wait_ge(d_ready, 1)
                with pool.Fori(0, NT // STEPS) as k:
                    part = wh[:, bass.ds(k * STEPS, STEPS), 0:F]
                    d = dcol[:, bass.ds(k * STEPS, STEPS)]
                    nc.gpsimd.tensor_tensor(part, part, d.unsqueeze(2).to_broadcast([P, STEPS, F]), ALU.mult)\
                        .then_inc(w_ready, 1)
                finish_all(BANDS, ROWS)

            with pool.If(safe(pool)):
                safe_path()
                pool.nop()
            with pool.Else():
                finish_all(NT, 1)
                pool.nop()
            pool.nop()

        @block.scalar
        def _(act):
            act.sem_inc(sums_copied, 2)
            act.sem_inc(s1_copied, 2)
            act.wait_ge(var_ready, 1)
            nc.scalar.activation(rstd[:, :], tmp2[:, :], ACT.Sqrt).then_inc(std_ready, 1)

            def copy_s1(g):
                act.wait_ge(s1_done, g + 1)
                nc.scalar.copy(rbc[:, g * GROUP * P:(g + 1) * GROUP * P], ps[:, 6 + g % 2, :]).then_inc(s1_copied, 1)

            for g in range(GROUPS):
                act.wait_ge(xt_ready, g + 1)
                nc.scalar.activation(ht[:, g % 2, :], ps[:, 4 + g % 2, :], ACT.Relu,
                                     accum_out=hsum[:, g:g + 1]).then_inc(ht_ready, 1)
                if g >= 1:
                    copy_s1(g - 1)
            copy_s1(GROUPS - 1)

            def safe_path():
                def form_gates(band, k):
                    act.wait_ge(raw_in[k % RAW_SLOTS], band * (CHUNKS // RAW_SLOTS * 16) + (k // RAW_SLOTS + 1) * 16)
                    if not (isinstance(band, int) and band * CHUNKS + k < GATE_SLOTS):
                        act.wait_ge(turned_ready, band * BAND_STEPS + (k - GATE_SLOTS + 1) * STEPS)
                    nc.scalar.activation(gate[:, k % GATE_SLOTS, :, :], raw[:, k % RAW_SLOTS, :, :], ACT.Exp,
                                         bias=bias[:, 2:3], scale=GATE_SCALE).then_inc(gate_ready, 1)

                def copy_sums(band, half):
                    act.wait_ge(weights_used, band * BAND_STEPS + (BAND_STEPS + WT_SLOTS))
                    act.wait_ge(hacc_free, band + 1)
                    nc.scalar.copy(hacc[:, half, :, :].rearrange("p (b t) f -> p b (t f)", b=2), acc[half])\
                        .then_inc(sums_copied, 1)

                def exps(band):
                    act.wait_ge(neg_ready, band + 1)
                    nc.scalar.activation(neg[:, :, :], neg[:, :, :], ACT.Exp).then_inc(exp_ready, 1)

                act.wait_ge(consts, 3)
                nc.scalar.activation(dcol[:, :], wh[:, :, F], ACT.Exp, bias=bias[:, 0:1], scale=SLOPE)\
                    .then_inc(d_ready, 1)
                nc.scalar.activation(beta[:, :], wh[:, :, F], ACT.Exp, bias=bias[:, 1:2], scale=1.0 - SLOPE)\
                    .then_inc(d_ready, 1)
                act.wait_ge(z_ready, 1)
                nc.scalar.activation(rbc[:, 0:BAND], rbc[:, 0:BAND], ACT.Exp, scale=SLOPE - 1.0).then_inc(r_ready, 1)
                for k in range(CHUNKS):
                    form_gates(0, k)
                    if k == 1:
                        act.wait_ge(z_ready, 2)
                        nc.scalar.activation(rbc[:, BAND:], rbc[:, BAND:], ACT.Exp, scale=SLOPE - 1.0)\
                            .then_inc(r_ready, 1)

                def band_of_gates(band, half):
                    for k in range(CHUNKS):
                        form_gates(band, k)
                        if k == CHUNKS // 2 - 1:
                            copy_sums(band - 1, 1 - half)
                    exps(band - 1)

                band_of_gates(1, 1)
                with act.Fori(1, BANDS // 2) as pair:
                    for half in range(2):
                        band_of_gates(pair * 2 + half, half)
                copy_sums(BANDS - 1, 1)
                exps(BANDS - 1)

            def general_path():
                def tile_of_rows(tile, half):
                    act.wait_ge(g_scores, tile + 1)
                    act.wait_ge(hacc_free, tile + 1)
                    nc.scalar.activation(scores, scores, ACT.Exp, bias=nmax[:, 0:1],
                                         accum_out=hacc[:, half, 0, F:FD]).then_inc(g_probs, 1)
                    act.wait_ge(g_used, tile * (NT // GATHER) + (NT // GATHER + WT_SLOTS))
                    nc.scalar.copy(hacc[:, half, 0, 0:F], acc[half][:, 0, 0:F]).then_inc(sums_copied, 1)
                    act.wait_ge(neg_ready, tile + 1)
                    nc.scalar.activation(neg[:, 0, :], neg[:, 0, :], ACT.Exp).then_inc(exp_ready, 1)

                with act.Fori(0, NT // 2) as pair:
                    for half in range(2):
                        tile_of_rows(pair * 2 + half, half)

            with act.If(safe(act)):
                safe_path()
                act.nop()
            with act.Else():
                general_path()
                act.nop()
            act.nop()

        @block.vector
        def _(dve):
            links = [0]

            def link(ins):
                links[0] += 1
                ins.then_inc(dve_chain, 1)
                dve.wait_ge(dve_chain, links[0])

            dve.sem_inc(wh_copied, 2)
            dve.wait_ge(a_in, 32)
            nc.vector.tensor_copy(a1bc[:, :], a12[:, 0:1].to_broadcast([P, P])).then_inc(a1_ready, 1)
            dve.wait_ge(wt_turned, 1)
            nc.vector.tensor_copy(wt[:, :], ps[:, 4, 0:P]).then_inc(wt_ready, 1)

            for k in range(4):
                n = NT // 4
                dve.wait_ge(x_in[k], 16)
                with dve.Fori(0, n // 4) as q:
                    for u in range(4):
                        t = bass.ds(q * 4 + (k * n + u), 1)
                        ins = nc.vector.bn_stats(stats[:, t, :].rearrange("p t s -> p (t s)"),
                                                 xs[:, t, :].rearrange("p t s -> p (t s)"))
                    ins.then_inc(stats_done, 1)
            dve.wait_ge(stats_done, NT // 4)
            nc.vector.tensor_tensor(tmp1[:, :], stats[:, :, 1], stats[:, :, 4], ALU.subtract)
            nc.vector.tensor_tensor(mean[:, :], stats[:, :, 1], stats[:, :, 4], ALU.add)
            link(nc.vector.tensor_tensor(tmp2[:, :], stats[:, :, 2], stats[:, :, 5], ALU.add))
            nc.vector.tensor_scalar(mean[:, :], mean[:, :], 0.5, None, ALU.mult)
            link(nc.vector.tensor_tensor(tmp1[:, :], tmp1[:, :], tmp1[:, :], ALU.mult))
            link(nc.vector.scalar_tensor_tensor(tmp2[:, :], tmp1[:, :], F / 4, tmp2[:, :], ALU.mult, ALU.add))
            nc.vector.tensor_scalar(tmp2[:, :], tmp2[:, :], 1.0 / F, LN_EPS, ALU.mult, ALU.add).then_inc(var_ready, 1)
            dve.wait_ge(wa_done, 1)
            nc.vector.tensor_copy(wa1[:, :], ps[:, 5, 0:P])
            nc.vector.tensor_copy(wext[:, F:FD], ps[:, 5, P:P + 1]).then_inc(wa_ready, 1)
            dve.wait_ge(std_ready, 1)
            link(nc.vector.reciprocal(rstd[:, :], rstd[:, :]))

            def normalise(g, slot):
                for u in range(GROUP):
                    t = g * GROUP + u
                    ins = nc.vector.tensor_scalar(xn[:, slot, u:u + 1, :].rearrange("p t f -> p (t f)"),
                                                  xs[:, bass.ds(t, 1), :].rearrange("p t f -> p (t f)"),
                                                  mean[:, bass.ds(t, 1)], rstd[:, bass.ds(t, 1)],
                                                  ALU.subtract, ALU.mult)
                ins.then_inc(xn_ready, 1)

            def copy_wh(g, slot):
                dve.wait_ge(wh_done, g + 1)
                nc.vector.tensor_scalar(wh[:, bass.ds(g * GROUP, GROUP), :].rearrange("p (b t) f -> p b (t f)", b=2),
                                        acc[slot], 1.0, None, ALU.mult).then_inc(wh_copied, 1)

            normalise(0, 0)
            normalise(1, 1)
            with dve.Fori(0, GROUPS // 2 - 1) as pair:
                for slot in range(2):
                    copy_wh(pair * 2 + slot, slot)
                    dve.wait_ge(xt_ready, pair * 2 + (slot + 1))
                    normalise(pair * 2 + (slot + 2), slot)
            copy_wh(GROUPS - 2, 0)
            copy_wh(GROUPS - 1, 1)
            dve.wait_ge(wh_copied, GROUPS + 2)

            nc.vector.tensor_scalar(tmp1[:, :], wh[:, :, F], -1.0, None, ALU.mult)
            link(nc.vector.tensor_reduce(ext[:, 0:1], wh[:, :, F], AX_X, ALU.max))
            nc.vector.tensor_reduce(ext[:, 1:2], tmp1[:, :], AX_X, ALU.max).then_inc(ext_ready, 1)
            dve.wait_ge(ht_ready, GROUPS)
            link(nc.vector.tensor_reduce(htot[:, :], hsum[:, :], AX_X, ALU.add))
            nc.vector.tensor_scalar(hmean[:, :], htot[:, 0:1].to_broadcast([P, P]), 1.0 / N, None, ALU.mult)\
                .then_inc(hmean_ready, 1)
            dve.wait_ge(gext_ready, 1)
            nc.vector.tensor_scalar(bias[:, 0:1], gext[:, 0:1], -SLOPE, None, ALU.mult)
            nc.vector.tensor_scalar(bias[:, 1:2], gext[:, 0:1], SLOPE - 1.0, None, ALU.mult)
            link(nc.vector.tensor_tensor(spread[:, :], gext[:, 0:1], gext[:, 1:2], ALU.add))
            nc.vector.tensor_scalar(flag[:, :], spread[:, :], SAFE_SPREAD, None, ALU.is_le).then_inc(flag_ready, 1)
            dve.wait_ge(mwh_done, 1)
            nc.vector.tensor_copy(mean_wh[:, :], ps[:, 4, 0:F]).then_inc(mwh_ready, 1)

            LINKS = 1
            base = links[0]

            def reciprocals(band, half, tiles, first_link, links_per_band):
                dve.wait_ge(sums_copied, band + 3)
                den = hacc[:, half, 0:tiles, F]
                nc.vector.tensor_scalar(empty[:, half, 0:tiles], den, 0.0, None, ALU.is_le)
                nc.vector.scalar_tensor_tensor(rden[:, half, 0:tiles], den, 0.0, den, ALU.is_le, ALU.add)\
                    .then_inc(dve_chain, 1)
                dve.wait_ge(dve_chain, band * links_per_band + (first_link + 1))
                nc.vector.reciprocal(rden[:, half, 0:tiles], rden[:, half, 0:tiles]).then_inc(rden_ready, 1)

            def safe_path():
                dve.wait_ge(s1_copied, GROUPS + 2)
                nc.vector.tensor_scalar(rbc[:, 0:BAND], rbc[:, 0:BAND], gext[:, 0:1], 0.0, ALU.add, ALU.max)\
                    .then_inc(z_ready, 1)
                nc.vector.tensor_scalar(rbc[:, BAND:], rbc[:, BAND:], gext[:, 0:1], 0.0, ALU.add, ALU.max)\
                    .then_inc(z_ready, 1)
                dve.wait_ge(d_ready, 2)
                dve.wait_ge(w_ready, NT // STEPS)
                nc.vector.tensor_copy(wh[:, :, F], dcol[:, :]).then_inc(w_ready, 1)

                def steps(band, first):
                    for u in range(PAIR):
                        jt = first + u
                        dve.wait_ge(turned_ready, band * BAND_STEPS + (jt + 1))
                        dve.wait_ge(weights_used, band * BAND_STEPS + (jt + 1))
                        nc.vector.scalar_tensor_tensor(
                            weights[:, u % WT_SLOTS, :], rbc[:, bass.ds(band * BAND, BAND)],
                            beta[:, bass.ds(jt, 1)], turned[u % WT_SLOTS], ALU.max, ALU.min)\
                            .then_inc(weights_ready, 1)

                dve.wait_ge(r_ready, 1)
                with dve.Fori(0, PAIRS) as pair:
                    steps(0, pair * PAIR)
                dve.wait_ge(r_ready, 2)

                def band_of_weights(band, half):
                    with dve.Fori(0, PAIRS // 2) as pair:
                        steps(band, pair * PAIR)
                    reciprocals(band - 1, 1 - half, ROWS, base, 1)
                    with dve.Fori(PAIRS // 2, PAIRS) as pair:
                        steps(band, pair * PAIR)

                band_of_weights(1, 1)
                with dve.Fori(1, BANDS // 2) as pair:
                    for half in range(2):
                        band_of_weights(pair * 2 + half, half)
                reciprocals(BANDS - 1, 1, ROWS, base, 1)

            def general_path():
                row = [P, GROUP, P]
                eye = identf[:, :].unsqueeze(1).to_broadcast(row)
                dve.sem_inc(g_adj_free, 1)
                dve.wait_ge(s1_copied, GROUPS + 2)
                link(nc.vector.memset(wt[:, :], 1.0))
                here = links[0]
                with dve.Fori(0, GROUPS) as g:
                    block_of_rbc = rbc[:, bass.ds(g * GROUP * P, GROUP * P)]

                    def chained(k, ins):
                        ins.then_inc(dve_chain, 1)
                        dve.wait_ge(dve_chain, g * 3 + (here + k))

                    chained(1, nc.vector.tensor_tensor(xn[:, 0, :, :], block_of_rbc.rearrange("p (t q) -> p t q", q=P),
                                                       eye, ALU.mult))
                    chained(2, nc.vector.tensor_reduce(s1col[:, bass.ds(g * GROUP, GROUP)], xn[:, 0, :, :],
                                                       AX_X, ALU.add))
                    nc.vector.tensor_tensor(xn[:, 1, :, :],
                                            wh[:, bass.ds(g * GROUP, GROUP), F:FD].to_broadcast(row),
                                            eye, ALU.mult).then_inc(g_diag, 1)
                    dve.wait_ge(g_spread, g + 1)
                    chained(3, nc.vector.tensor_scalar(block_of_rbc, ps[:, 4, :], 1.0, None, ALU.mult))
                start = here + 3 * GROUPS
                TILE_LINKS = 6

                def tile_of_rows(tile, half):
                    def chained(k, ins):
                        ins.then_inc(dve_chain, 1)
                        dve.wait_ge(dve_chain, tile * TILE_LINKS + (start + k))

                    dve.wait_ge(g_used, tile * (NT // GATHER) + WT_SLOTS)
                    chained(1, nc.vector.tensor_scalar(scores, rbc[:, :], s1col[:, bass.ds(tile, 1)], None, ALU.add))
                    chained(2, nc.vector.scalar_tensor_tensor(scores, scores, SLOPE, scores, ALU.mult, ALU.max))
                    dve.wait_ge(g_adj, tile * 16 + 16)
                    chained(3, nc.vector.scalar_tensor_tensor(scores, adj_rows, 0.0, scores, ALU.is_gt, ALU.mult))
                    chained(4, nc.vector.tensor_scalar(adj_rows.bitcast(F32), adj_rows, 0.0, MASKED,
                                                       ALU.is_le, ALU.mult))
                    chained(5, nc.vector.tensor_tensor(scores, scores, adj_rows.bitcast(F32), ALU.add))
                    dve.sem_inc(g_adj_free, 1)
                    nc.vector.tensor_reduce(nmax[:, :], scores, AX_X, ALU.max, negate=True).then_inc(g_scores, 1)
                    for q in range(NT // GATHER):
                        dve.wait_ge(g_turned, tile * (NT // GATHER) + (q + 1))
                        dve.wait_ge(g_used, tile * (NT // GATHER) + (q + 1))
                        nc.vector.tensor_copy(weights[:, q % WT_SLOTS, :], ps[:, 4 + q % WT_SLOTS, :])\
                            .then_inc(g_copied, 1)
                    reciprocals(tile, half, 1, start + 5, TILE_LINKS)

                with dve.Fori(0, NT // 2) as pair:
                    for half in range(2):
                        tile_of_rows(pair * 2 + half, half)

            with dve.If(safe(dve)):
                safe_path()
                dve.nop()
            with dve.Else():
                general_path()
                dve.nop()
            dve.nop()

        @block.tensor
        def _(pe):
            pe.wait_ge(consts, 3)
            pe.wait_ge(w_in, 16)
            nc.tensor.transpose(ps[:, 4, 0:P], wext[:, 0:F], identf[:, :]).then_inc(wt_turned, 1)
            pe.wait_ge(wt_ready, 1)
            pe.wait_ge(a1_ready, 1)
            nc.tensor.matmul(ps[:, 5, 0:P], wt[:, :], a1bc[:, :], start=True, stop=True)
            nc.tensor.matmul(ps[:, 5, P:P + 1], wt[:, :], a12[:, 1:2], start=True, stop=True).then_inc(wa_done, 1)

            def turn(g, slot):
                pe.wait_ge(xn_ready, g + 1)
                for u in range(GROUP):
                    ins = nc.tensor.transpose(ps[:, 4 + slot, u * P:(u + 1) * P], xn[:, slot, u, :], identf[:, :])
                ins.then_inc(xt_ready, 1)

            def products(g, slot):
                pe.wait_ge(ht_ready, g + 1)
                pe.wait_ge(wh_copied, g + 1)
                for u in range(GROUP):
                    ins = nc.tensor.matmul(acc[slot][:, u // 2, (u % 2) * FD:(u % 2 + 1) * FD],
                                           ht[:, slot, u * P:(u + 1) * P], wext[:, :], start=True, stop=True)
                ins.then_inc(wh_done, 1)
                pe.wait_ge(s1_copied, g + 1)
                nc.tensor.matmul(ps[:, 6 + slot, :], wa1[:, :], ht[:, slot, :], start=True, stop=True)\
                    .then_inc(s1_done, 1)

            pe.wait_ge(wa_ready, 1)
            turn(0, 0)
            with pe.Fori(0, GROUPS // 2 - 1) as pair:
                turn(pair * 2 + 1, 1)
                products(pair * 2, 0)
                turn(pair * 2 + 2, 0)
                products(pair * 2 + 1, 1)
            turn(GROUPS - 1, 1)
            products(GROUPS - 2, 0)
            products(GROUPS - 1, 1)
            pe.wait_ge(hmean_ready, 1)
            nc.tensor.matmul(ps[:, 4, 0:F], hmean[:, :], wext[:, 0:F], start=True, stop=True).then_inc(mwh_done, 1)

            def safe_path():
                pe.wait_ge(mwh_ready, 1)
                pe.wait_ge(wh_copied, GROUPS + 2)
                pe.wait_ge(s1_copied, GROUPS + 2)

                def turn_gates(band, pair, u):
                    k, inside = u // STEPS % GATE_SLOTS, u % STEPS
                    if inside == 0:
                        pe.wait_ge(gate_ready, band * CHUNKS + pair * 2 + (u // STEPS + 1))
                    for r in range(ROWS):
                        ins = nc.tensor.transpose(turned[u % WT_SLOTS][:, r * P:(r + 1) * P],
                                                  gate[:, k, r, inside * P:(inside + 1) * P], identb[:, :])
                    ins.then_inc(turned_ready, 1)

                def multiply(band, pair, u, half, last):
                    pe.wait_ge(weights_ready, band * BAND_STEPS + pair * PAIR + (u + 1))
                    for r in range(ROWS):
                        ins = nc.tensor.matmul(acc[half][:, r // 2, (r % 2) * FD:(r % 2 + 1) * FD],
                                               weights[:, u % WT_SLOTS, r * P:(r + 1) * P],
                                               wh[:, bass.ds(pair * PAIR + u, 1), :].rearrange("p t f -> p (t f)"),
                                               start=False, stop=last and r % 2 == 1, skip_group_check=True)
                    ins.then_inc(weights_used, 1)

                def band_of_products(band, half, last=False):
                    pe.wait_ge(sums_copied, band + 1)
                    for b in range(2):
                        nc.tensor.matmul(acc[half][:, b, :], zeros[:, 0:P], zeros[:, :], start=True, stop=False,
                                         skip_group_check=True)
                    with pe.Fori(0, PAIRS - last) as pair:
                        for u in range(PAIR):
                            turn_gates(band, pair, u + LEAD)
                            multiply(band, pair, u, half, False)
                    if last:
                        for u in range(PAIR):
                            if u + LEAD < PAIR:
                                turn_gates(band, PAIRS - 1, u + LEAD)
                            multiply(band, PAIRS - 1, u, half, u == PAIR - 1)

                for u in range(LEAD):
                    turn_gates(0, 0, u)
                pe.wait_ge(w_ready, NT // STEPS + 1)
                with pe.Fori(0, BANDS // 2 - 1) as pair:
                    for half in range(2):
                        band_of_products(pair * 2 + half, half)
                band_of_products(BANDS - 2, 0)
                band_of_products(BANDS - 1, 1, last=True)

            def general_path():
                pe.sem_inc(g_used, WT_SLOTS)
                pe.wait_ge(mwh_ready, 1)
                with pe.Fori(0, GROUPS) as g:
                    pe.wait_ge(g_diag, g + 1)
                    nc.tensor.matmul(ps[:, 4, :], wt[:, :], xn[:, 1, :, :].rearrange("p t q -> p (t q)"),
                                     start=True, stop=True).then_inc(g_spread, 1)

                def turn_probs(q):
                    for u in range(GATHER):
                        jt = q * GATHER + u
                        ins = nc.tensor.transpose(ps[:, 4 + q % WT_SLOTS, u * P:(u + 1) * P],
                                                  scores[:, jt * P:(jt + 1) * P], identf[:, :])
                    ins.then_inc(g_turned, 1)

                def tile_of_rows(tile, half):
                    pe.wait_ge(g_probs, tile + 1)
                    pe.wait_ge(sums_copied, tile + 1)
                    n = NT // GATHER
                    turn_probs(0)
                    for q in range(n):
                        if q + 1 < n:
                            turn_probs(q + 1)
                        pe.wait_ge(g_copied, tile * n + (q + 1))
                        for u in range(GATHER):
                            ins = nc.tensor.matmul(acc[half][:, 0, 0:F], weights[:, q % WT_SLOTS, u * P:(u + 1) * P],
                                                   wh[:, q * GATHER + u, 0:F],
                                                   start=q + u == 0, stop=q == n - 1 and u == GATHER - 1)
                        ins.then_inc(g_used, 1)

                with pe.Fori(0, NT // 2) as pair:
                    for half in range(2):
                        tile_of_rows(pair * 2 + half, half)

            pe.sem_inc(weights_used, WT_SLOTS)
            with pe.If(safe(pe)):
                safe_path()
                pe.nop()
            with pe.Else():
                general_path()
                pe.nop()
            pe.nop()


_INS = ["x", "adj", "L0_gnn_W", "L0_gnn_a"]
_OUT = ((8192, 128), "float32")


def kernel(**inputs):
    import numpy as _np
    import concourse.bacc as _bacc
    from concourse import mybir as _mybir
    from concourse.bass_utils import run_bass_kernel_spmd as _run

    nc = _bacc.Bacc("TRN2", target_bir_lowering=False, num_devices=1)
    arrays, args = {}, []
    for name in _INS:
        v = _np.ascontiguousarray(inputs[name])
        arrays[f"in_{name}"] = v
        args.append(nc.dram_tensor(f"in_{name}", v.shape, _mybir.dt.from_np(v.dtype), kind="ExternalInput").ap())
    shape, dtype = _OUT
    args.append(nc.dram_tensor("out_x", shape, _mybir.dt.from_np(_np.dtype(dtype)), kind="ExternalOutput").ap())
    graph_attention(nc, *args)
    r = _run(nc, [arrays], core_ids=[0])
    return r.results[0]["out_x"]
```

```python
from contextlib import ExitStack

import concourse.bass as bass
from concourse import mybir

ALU = mybir.AluOpType
ACT = mybir.ActivationFunctionType
AX_X = mybir.AxisListType.X
F32 = mybir.dt.float32
BF16 = mybir.dt.bfloat16
I32 = mybir.dt.int32
U8 = mybir.dt.uint8

P = 128
SLOPE = 0.2
MASKED = -9000000000000000.0
LN_EPS = 1e-5
SAFE_SPREAD = 60.0
GATE_SCALE = 280.0
GATE_BIAS = -140.0

QUAD = 4
PACK = 2
ROWS = QUAD
CHUNK = 1024
STEPS = CHUNK // P
RAW_SLOTS = 4
GATE_SLOTS = 2
TURNED_SLOTS = 2
WT_SLOTS = 4
GROUP = QUAD


def graph_attention(nc, x, adj, w, a, out):
    N, F = x.shape
    NT = N // P
    BANDS = N // (ROWS * P)
    BAND = ROWS * P
    CHUNKS = N // CHUNK
    GROUPS = NT // GROUP
    FD = F + 1
    PAIR = 2 * STEPS
    PAIRS = CHUNKS // 2
    BAND_STEPS = NT
    QUADS = CHUNK // (QUAD * P)
    GATHER = QUAD
    assert F == P and CHUNKS % RAW_SLOTS == 0 and QUAD % WT_SLOTS == 0 and BANDS % 2 == 0

    with ExitStack() as ctx:
        def sb(name, shape, dt=F32):
            return ctx.enter_context(nc.sbuf_tensor(name, shape, dt))

        def sem(name):
            return ctx.enter_context(nc.semaphore(name))

        raw = sb("raw", [P, RAW_SLOTS, ROWS, CHUNK], I32)
        gate = sb("gate", [P, GATE_SLOTS, ROWS, CHUNK], U8)
        xs = sb("xs", [P, NT, F])
        rbc = sb("rbc", [P, N])
        wh = sb("wh", [P, NT, FD])
        weights = sb("weights", [P, WT_SLOTS, BAND])
        hacc = sb("hacc", [P, 2, ROWS, FD])
        obuf = sb("obuf", [P, 2, ROWS, F])
        hp = sb("hp", [P, ROWS, F])
        neg = sb("neg", [P, ROWS, F])
        xn = weights[:, 0:2, :].rearrange("p s (t f) -> p s t f", f=F)
        ht = weights[:, 2:4, :]
        identf = sb("identf", [P, P])
        identb = sb("identb", [P, P], BF16)
        zeros = sb("zeros", [P, 2 * FD], BF16)
        wext = sb("wext", [P, FD])
        wt = sb("wt", [P, P])
        wa1 = sb("wa1", [P, P])
        a12 = sb("a12", [P, 2])
        a1bc = sb("a1bc", [P, P])
        stats = sb("stats", [P, NT, 6])
        mean = sb("mean", [P, NT])
        rstd = sb("rstd", [P, NT])
        tmp1 = sb("tmp1", [P, NT])
        tmp2 = sb("tmp2", [P, NT])
        hsum = sb("hsum", [P, GROUPS])
        htot = sb("htot", [P, 1])
        hmean = sb("hmean", [P, P])
        mean_wh = sb("mean_wh", [P, F])
        ext = sb("ext", [P, 2])
        gext = sb("gext", [P, 2])
        spread = sb("spread", [P, 1])
        flag = sb("flag", [P, 1], I32)
        bias = sb("bias", [P, 3])
        dcol = sb("dcol", [P, NT])
        beta = sb("beta", [P, NT])
        empty = sb("empty", [P, 2, ROWS])
        rden = sb("rden", [P, 2, ROWS])
        s1col = sb("s1col", [P, NT])
        nmax = sb("nmax", [P, 1])

        ps = ctx.enter_context(nc.psum_tensor("ps", [P, 8, 512], F32))
        acc = [ps[:, 2 * k:2 * k + 2, 0:2 * FD] for k in range(2)]
        turned = [ps[:, 4 + k, :].bitcast(BF16).rearrange("p (c i) -> p c i", i=BAND) for k in range(TURNED_SLOTS)]
        turned_bytes = [ps[:, 4 + k, :].bitcast(U8).rearrange("p (c i b) -> p c i b", i=BAND, b=PACK)
                        for k in range(TURNED_SLOTS)]

        w_in, a_in = sem("w_in"), sem("a_in")
        x_in = [sem(f"x_in{k}") for k in range(4)]
        raw_in = [sem(f"raw_in{k}") for k in range(RAW_SLOTS)]
        out_done = [sem(f"out_done{k}") for k in range(2)]
        consts = sem("consts")
        dve_chain, pool_chain, stats_done = sem("dve_chain"), sem("pool_chain"), sem("stats_done")
        wt_turned, wt_ready, a1_ready, wa_done, wa_ready = (
            sem("wt_turned"), sem("wt_ready"), sem("a1_ready"), sem("wa_done"), sem("wa_ready"))
        var_ready, std_ready = sem("var_ready"), sem("std_ready")
        xn_ready, xt_ready, ht_ready = sem("xn_ready"), sem("xt_ready"), sem("ht_ready")
        wh_done, wh_copied = sem("wh_done"), sem("wh_copied")
        s1_done, s1_copied = sem("s1_done"), sem("s1_copied")
        hmean_ready, mwh_done, mwh_ready = sem("hmean_ready"), sem("mwh_done"), sem("mwh_ready")
        ext_ready, gext_ready, flag_ready = sem("ext_ready"), sem("gext_ready"), sem("flag_ready")
        d_ready, z_ready, r_ready, w_ready = sem("d_ready"), sem("z_ready"), sem("r_ready"), sem("w_ready")
        gate_ready = sem("gate_ready")
        turned_ready = sem("turned_ready")
        weights_ready = sem("weights_ready")
        weights_used = sem("weights_used")
        sums_copied = sem("sums_copied")
        hacc_free = sem("hacc_free")
        rden_ready, neg_ready, exp_ready, out_ready = (
            sem("rden_ready"), sem("neg_ready"), sem("exp_ready"), sem("out_ready"))
        g_diag, g_spread = sem("g_diag"), sem("g_spread")
        g_adj, g_adj_free = sem("g_adj"), sem("g_adj_free")
        g_scores, g_probs = sem("g_scores"), sem("g_probs")
        g_turned, g_copied, g_used = sem("g_turned"), sem("g_copied"), sem("g_used")

        scores = raw[:, 2:4, :, :].rearrange("p s t j -> p (s t j)").bitcast(F32)
        adj_rows = raw[:, 0:2, :, :].rearrange("p s t j -> p (s t j)")
        x_blocks = x.rearrange("(k p b) f -> p k b f", p=P, b=QUAD)
        adj_blocks = adj.rearrange("(k p b) j -> p k b j", p=P, b=QUAD)
        out_blocks = out.rearrange("(k p b) f -> p k b f", p=P, b=QUAD)

        def safe(eng):
            eng.wait_ge(flag_ready, 1)
            return eng.value_load(flag[0:1, 0:1], min_val=0, max_val=1) == 1

        block = ctx.enter_context(nc.Block())

        @block.sync
        def _(sp):
            sp.dma_start(wext[:, 0:F], w).then_inc(w_in, 16)
            for k in range(2):
                sp.dma_start(a12[:, k:k + 1], a[k * F:(k + 1) * F, :]).then_inc(a_in, 16)
            for k in range(4):
                n = NT // 4
                sp.dma_start(xs[:, k * n:(k + 1) * n, :].rearrange("p (k b) f -> p k b f", b=QUAD),
                             x_blocks[:, k * n // QUAD:(k + 1) * n // QUAD, :, :]).then_inc(x_in[k], 16)

            def load(band, chunk, slot):
                rows = adj_blocks[:, bass.ds(band, 1), :, chunk * CHUNK:(chunk + 1) * CHUNK]
                sp.dma_start(raw[:, slot, :, :], rows.rearrange("p k b j -> p (k b) j")).then_inc(raw_in[slot], 16)

            for k in range(RAW_SLOTS):
                load(0, k, k)

            def safe_path():
                for k in range(RAW_SLOTS, CHUNKS):
                    sp.wait_ge(gate_ready, k - RAW_SLOTS + 1)
                    load(0, k, k % RAW_SLOTS)
                with sp.Fori(1, BANDS) as band:
                    for k in range(CHUNKS):
                        sp.wait_ge(gate_ready, band * CHUNKS + (k - RAW_SLOTS + 1))
                        load(band, k, k % RAW_SLOTS)

            def general_path():
                for k in range(RAW_SLOTS):
                    sp.wait_ge(raw_in[k], 16)
                with sp.Fori(0, BANDS) as k:
                    for b in range(QUAD):
                        sp.wait_ge(g_adj_free, k * QUAD + (b + 1))
                        sp.dma_start(adj_rows, adj_blocks[:, bass.ds(k, 1), b, :].rearrange("p k j -> p (k j)"))\
                            .then_inc(g_adj, 16)

            with sp.If(safe(sp)):
                safe_path()
                sp.nop()
            with sp.Else():
                general_path()
                sp.nop()
            sp.nop()

        @block.gpsimd
        def _(pool):
            links = [0]

            def link(ins):
                links[0] += 1
                ins.then_inc(pool_chain, 1)
                pool.wait_ge(pool_chain, links[0])

            pool.sem_inc(hacc_free, 2)
            link(nc.gpsimd.memset(identf[:, :], 0.0))
            link(nc.gpsimd.affine_select(out=identf[:, :], in_=identf[:, :], compare_op=ALU.not_equal, fill=1.0,
                                         base=0, pattern=[[-1, P]], channel_multiplier=1))
            nc.gpsimd.tensor_copy(identb[:, :], identf[:, :]).then_inc(consts, 1)
            nc.gpsimd.memset(bias[:, 2:3], GATE_BIAS).then_inc(consts, 1)
            nc.gpsimd.memset(zeros[:, :], 0.0).then_inc(consts, 1)
            pool.wait_ge(ext_ready, 1)
            nc.gpsimd.partition_all_reduce(gext[:, :], ext[:, :], P, bass.bass_isa.ReduceOp.max)\
                .then_inc(gext_ready, 1)

            LINKS = 4
            base = links[0]

            def finish_band(band, half, tiles, first, to, stored=None):
                done = [0]

                def chained(ins):
                    done[0] += 1
                    ins.then_inc(pool_chain, 1)
                    pool.wait_ge(pool_chain, band * LINKS + (base + done[0]))

                h, n, o = hp[:, 0:tiles, :], neg[:, 0:tiles, :], obuf[:, half, 0:tiles, :]
                row = [P, tiles, F]
                pool.wait_ge(rden_ready, band + 1)
                nc.gpsimd.tensor_tensor(n, empty[:, half, 0:tiles].unsqueeze(2).to_broadcast(row),
                                        mean_wh[:, :].unsqueeze(1).to_broadcast(row), ALU.mult)
                chained(nc.gpsimd.tensor_tensor(h, hacc[:, half, 0:tiles, 0:F],
                                                rden[:, half, 0:tiles].unsqueeze(2).to_broadcast(row), ALU.mult))
                chained(nc.gpsimd.tensor_tensor(h, h, n, ALU.add))
                pool.sem_inc(hacc_free, 1)
                nc.gpsimd.tensor_scalar(n, h, 0.0, None, ALU.min).then_inc(neg_ready, 1)
                chained(nc.gpsimd.tensor_scalar(h, h, 0.0, -1.0, ALU.max, ALU.add))
                if stored is not None:
                    pool.wait_ge(out_done[half], stored * 16)
                chained(nc.gpsimd.tensor_tensor(o, h, xs[:, bass.ds(first, tiles), :], ALU.add))
                pool.wait_ge(exp_ready, band + 1)
                nc.gpsimd.tensor_tensor(o, o, n, ALU.add).then_inc(out_ready, 1)
                pool.wait_ge(out_ready, band + 1)
                pool.dma_start(to, o).then_inc(out_done[half], 16)

            def finish_bands():
                def rows(band):
                    return out_blocks[:, bass.ds(band, 1), :, :].rearrange("p k b f -> p (k b) f")

                for half in range(2):
                    finish_band(half, half, ROWS, half * ROWS, rows(half))
                with pool.Fori(1, BANDS // 2) as pair:
                    for half in range(2):
                        finish_band(pair * 2 + half, half, ROWS, pair * (2 * ROWS) + half * ROWS,
                                    rows(pair * 2 + half), stored=pair)
                for half in range(2):
                    pool.wait_ge(out_done[half], 16 * (BANDS // 2))

            def finish_tiles():
                for b in range(QUAD):
                    finish_band(b, b % 2, 1, b, out_blocks[:, 0:1, b, :], stored=b // 2 or None)
                with pool.Fori(1, BANDS) as k:
                    for b in range(QUAD):
                        finish_band(k * QUAD + b, b % 2, 1, k * QUAD + b, out_blocks[:, bass.ds(k, 1), b, :],
                                    stored=k * 2 + b // 2)
                for half in range(2):
                    pool.wait_ge(out_done[half], 16 * (NT // 2))

            def safe_path():
                pool.wait_ge(d_ready, 1)
                with pool.Fori(0, NT // STEPS) as k:
                    part = wh[:, bass.ds(k * STEPS, STEPS), 0:F]
                    d = dcol[:, bass.ds(k * STEPS, STEPS)]
                    nc.gpsimd.tensor_tensor(part, part, d.unsqueeze(2).to_broadcast([P, STEPS, F]), ALU.mult)\
                        .then_inc(w_ready, 1)
                pool.wait_ge(mwh_ready, 1)
                finish_bands()

            with pool.If(safe(pool)):
                safe_path()
                pool.nop()
            with pool.Else():
                pool.wait_ge(mwh_ready, 1)
                finish_tiles()
                pool.nop()
            pool.nop()

        @block.scalar
        def _(act):
            act.sem_inc(sums_copied, 2)
            act.sem_inc(s1_copied, 2)
            act.wait_ge(var_ready, 1)
            nc.scalar.activation(rstd[:, :], tmp2[:, :], ACT.Sqrt).then_inc(std_ready, 1)

            def copy_s1(g):
                act.wait_ge(s1_done, g + 1)
                nc.scalar.copy(rbc[:, g * GROUP * P:(g + 1) * GROUP * P], ps[:, 6 + g % 2, :]).then_inc(s1_copied, 1)

            for g in range(GROUPS):
                act.wait_ge(xt_ready, g + 1)
                nc.scalar.activation(ht[:, g % 2, :], ps[:, 4 + g % 2, :], ACT.Relu,
                                     accum_out=hsum[:, g:g + 1]).then_inc(ht_ready, 1)
                if g >= 1:
                    copy_s1(g - 1)
            copy_s1(GROUPS - 1)

            def safe_path():
                def form_gates(band, k):
                    act.wait_ge(raw_in[k % RAW_SLOTS], band * (CHUNKS // RAW_SLOTS * 16) + (k // RAW_SLOTS + 1) * 16)
                    if not (isinstance(band, int) and band * CHUNKS + k < GATE_SLOTS):
                        act.wait_ge(turned_ready, band * (CHUNKS * QUADS) + (k - GATE_SLOTS + 1) * QUADS)
                    nc.scalar.activation(gate[:, k % GATE_SLOTS, :, :], raw[:, k % RAW_SLOTS, :, :], ACT.Sigmoid,
                                         bias=bias[:, 2:3], scale=GATE_SCALE).then_inc(gate_ready, 1)

                def copy_sums(band, half):
                    act.wait_ge(weights_used, band * BAND_STEPS + (BAND_STEPS + WT_SLOTS))
                    act.wait_ge(hacc_free, band + 1)
                    nc.scalar.copy(hacc[:, half, :, :].rearrange("p (b t) f -> p b (t f)", b=2), acc[half])\
                        .then_inc(sums_copied, 1)

                def exps(band):
                    act.wait_ge(neg_ready, band + 1)
                    nc.scalar.activation(neg[:, :, :], neg[:, :, :], ACT.Exp).then_inc(exp_ready, 1)

                act.wait_ge(consts, 3)
                nc.scalar.activation(dcol[:, :], wh[:, :, F], ACT.Exp, bias=bias[:, 0:1], scale=SLOPE)\
                    .then_inc(d_ready, 1)
                nc.scalar.activation(beta[:, :], wh[:, :, F], ACT.Exp, bias=bias[:, 1:2], scale=1.0 - SLOPE)\
                    .then_inc(d_ready, 1)
                act.wait_ge(z_ready, 1)
                nc.scalar.activation(rbc[:, 0:BAND], rbc[:, 0:BAND], ACT.Exp, scale=SLOPE - 1.0).then_inc(r_ready, 1)
                for k in range(CHUNKS):
                    form_gates(0, k)
                    if k == 1:
                        act.wait_ge(z_ready, 2)
                        nc.scalar.activation(rbc[:, BAND:], rbc[:, BAND:], ACT.Exp, scale=SLOPE - 1.0)\
                            .then_inc(r_ready, 1)

                def band_of_gates(band, half):
                    for k in range(CHUNKS):
                        form_gates(band, k)
                        if k == CHUNKS // 2 - 1:
                            copy_sums(band - 1, 1 - half)
                    exps(band - 1)

                band_of_gates(1, 1)
                with act.Fori(1, BANDS // 2) as pair:
                    for half in range(2):
                        band_of_gates(pair * 2 + half, half)
                copy_sums(BANDS - 1, 1)
                exps(BANDS - 1)

            def general_path():
                def tile_of_rows(tile, half):
                    act.wait_ge(g_scores, tile + 1)
                    act.wait_ge(hacc_free, tile + 1)
                    nc.scalar.activation(scores, scores, ACT.Exp, bias=nmax[:, 0:1],
                                         accum_out=hacc[:, half, 0, F:FD]).then_inc(g_probs, 1)
                    act.wait_ge(g_used, tile * (NT // GATHER) + (NT // GATHER + WT_SLOTS))
                    nc.scalar.copy(hacc[:, half, 0, 0:F], acc[half][:, 0, 0:F]).then_inc(sums_copied, 1)
                    act.wait_ge(neg_ready, tile + 1)
                    nc.scalar.activation(neg[:, 0, :], neg[:, 0, :], ACT.Exp).then_inc(exp_ready, 1)

                with act.Fori(0, NT // 2) as pair:
                    for half in range(2):
                        tile_of_rows(pair * 2 + half, half)

            with act.If(safe(act)):
                safe_path()
                act.nop()
            with act.Else():
                general_path()
                act.nop()
            act.nop()

        @block.vector
        def _(dve):
            links = [0]

            def link(ins):
                links[0] += 1
                ins.then_inc(dve_chain, 1)
                dve.wait_ge(dve_chain, links[0])

            dve.sem_inc(wh_copied, 2)
            dve.wait_ge(a_in, 32)
            nc.vector.tensor_copy(a1bc[:, :], a12[:, 0:1].to_broadcast([P, P])).then_inc(a1_ready, 1)
            dve.wait_ge(wt_turned, 1)
            nc.vector.tensor_copy(wt[:, :], ps[:, 4, 0:P]).then_inc(wt_ready, 1)

            for k in range(4):
                n = NT // 4
                dve.wait_ge(x_in[k], 16)
                with dve.Fori(0, n // 4) as q:
                    for u in range(4):
                        t = bass.ds(q * 4 + (k * n + u), 1)
                        ins = nc.vector.bn_stats(stats[:, t, :].rearrange("p t s -> p (t s)"),
                                                 xs[:, t, :].rearrange("p t s -> p (t s)"))
                    ins.then_inc(stats_done, 1)
            dve.wait_ge(stats_done, NT // 4)
            nc.vector.tensor_tensor(tmp1[:, :], stats[:, :, 1], stats[:, :, 4], ALU.subtract)
            nc.vector.tensor_tensor(mean[:, :], stats[:, :, 1], stats[:, :, 4], ALU.add)
            link(nc.vector.tensor_tensor(tmp2[:, :], stats[:, :, 2], stats[:, :, 5], ALU.add))
            nc.vector.tensor_scalar(mean[:, :], mean[:, :], 0.5, None, ALU.mult)
            link(nc.vector.tensor_tensor(tmp1[:, :], tmp1[:, :], tmp1[:, :], ALU.mult))
            link(nc.vector.scalar_tensor_tensor(tmp2[:, :], tmp1[:, :], F / 4, tmp2[:, :], ALU.mult, ALU.add))
            nc.vector.tensor_scalar(tmp2[:, :], tmp2[:, :], 1.0 / F, LN_EPS, ALU.mult, ALU.add).then_inc(var_ready, 1)
            dve.wait_ge(wa_done, 1)
            nc.vector.tensor_copy(wa1[:, :], ps[:, 5, 0:P])
            nc.vector.tensor_copy(wext[:, F:FD], ps[:, 5, P:P + 1]).then_inc(wa_ready, 1)
            dve.wait_ge(std_ready, 1)
            link(nc.vector.reciprocal(rstd[:, :], rstd[:, :]))

            def normalise(g, slot):
                for u in range(GROUP):
                    t = g * GROUP + u
                    ins = nc.vector.tensor_scalar(xn[:, slot, u:u + 1, :].rearrange("p t f -> p (t f)"),
                                                  xs[:, bass.ds(t, 1), :].rearrange("p t f -> p (t f)"),
                                                  mean[:, bass.ds(t, 1)], rstd[:, bass.ds(t, 1)],
                                                  ALU.subtract, ALU.mult)
                ins.then_inc(xn_ready, 1)

            def copy_wh(g, slot):
                dve.wait_ge(wh_done, g + 1)
                nc.vector.tensor_scalar(wh[:, bass.ds(g * GROUP, GROUP), :].rearrange("p (b t) f -> p b (t f)", b=2),
                                        acc[slot], 1.0, None, ALU.mult).then_inc(wh_copied, 1)

            normalise(0, 0)
            normalise(1, 1)
            with dve.Fori(0, GROUPS // 2 - 1) as pair:
                for slot in range(2):
                    copy_wh(pair * 2 + slot, slot)
                    dve.wait_ge(xt_ready, pair * 2 + (slot + 1))
                    normalise(pair * 2 + (slot + 2), slot)
            copy_wh(GROUPS - 2, 0)
            copy_wh(GROUPS - 1, 1)
            dve.wait_ge(wh_copied, GROUPS + 2)

            nc.vector.tensor_scalar(tmp1[:, :], wh[:, :, F], -1.0, None, ALU.mult)
            link(nc.vector.tensor_reduce(ext[:, 0:1], wh[:, :, F], AX_X, ALU.max))
            nc.vector.tensor_reduce(ext[:, 1:2], tmp1[:, :], AX_X, ALU.max).then_inc(ext_ready, 1)
            dve.wait_ge(ht_ready, GROUPS)
            link(nc.vector.tensor_reduce(htot[:, :], hsum[:, :], AX_X, ALU.add))
            nc.vector.tensor_scalar(hmean[:, :], htot[:, 0:1].to_broadcast([P, P]), 1.0 / N, None, ALU.mult)\
                .then_inc(hmean_ready, 1)
            dve.wait_ge(gext_ready, 1)
            nc.vector.tensor_scalar(bias[:, 0:1], gext[:, 0:1], -SLOPE, None, ALU.mult)
            nc.vector.tensor_scalar(bias[:, 1:2], gext[:, 0:1], SLOPE - 1.0, None, ALU.mult)
            link(nc.vector.tensor_tensor(spread[:, :], gext[:, 0:1], gext[:, 1:2], ALU.add))
            nc.vector.tensor_scalar(flag[:, :], spread[:, :], SAFE_SPREAD, None, ALU.is_le).then_inc(flag_ready, 1)
            dve.wait_ge(mwh_done, 1)
            nc.vector.tensor_copy(mean_wh[:, :], ps[:, 4, 0:F]).then_inc(mwh_ready, 1)

            LINKS = 1
            base = links[0]

            def reciprocals(band, half, tiles, first_link, links_per_band):
                dve.wait_ge(sums_copied, band + 3)
                den = hacc[:, half, 0:tiles, F]
                nc.vector.tensor_scalar(empty[:, half, 0:tiles], den, 0.0, None, ALU.is_le)
                nc.vector.scalar_tensor_tensor(rden[:, half, 0:tiles], den, 0.0, den, ALU.is_le, ALU.add)\
                    .then_inc(dve_chain, 1)
                dve.wait_ge(dve_chain, band * links_per_band + (first_link + 1))
                nc.vector.reciprocal(rden[:, half, 0:tiles], rden[:, half, 0:tiles]).then_inc(rden_ready, 1)

            def safe_path():
                dve.wait_ge(s1_copied, GROUPS + 2)
                nc.vector.tensor_scalar(rbc[:, 0:BAND], rbc[:, 0:BAND], gext[:, 0:1], 0.0, ALU.add, ALU.max)\
                    .then_inc(z_ready, 1)
                nc.vector.tensor_scalar(rbc[:, BAND:], rbc[:, BAND:], gext[:, 0:1], 0.0, ALU.add, ALU.max)\
                    .then_inc(z_ready, 1)
                dve.wait_ge(d_ready, 2)
                dve.wait_ge(w_ready, NT // STEPS)
                nc.vector.tensor_copy(wh[:, :, F], dcol[:, :]).then_inc(w_ready, 1)

                def steps(band, pair):
                    for u in range(PAIR):
                        jt = pair * PAIR + u
                        if u % QUAD == 0:
                            dve.wait_ge(turned_ready, band * (CHUNKS * QUADS) + pair * (2 * QUADS) + (u // QUAD + 1))
                        dve.wait_ge(weights_used, band * BAND_STEPS + (jt + 1))
                        nc.vector.scalar_tensor_tensor(
                            weights[:, u % WT_SLOTS, :], rbc[:, bass.ds(band * BAND, BAND)],
                            beta[:, bass.ds(jt, 1)], turned_bytes[u // QUAD % TURNED_SLOTS][:, u % QUAD // PACK, :, u % PACK],
                            ALU.max, ALU.min)\
                            .then_inc(weights_ready, 1)

                dve.wait_ge(r_ready, 1)
                with dve.Fori(0, PAIRS) as pair:
                    steps(0, pair)
                dve.wait_ge(r_ready, 2)

                def band_of_weights(band, half):
                    with dve.Fori(0, PAIRS // 2) as pair:
                        steps(band, pair)
                    reciprocals(band - 1, 1 - half, ROWS, base, 1)
                    with dve.Fori(PAIRS // 2, PAIRS) as pair:
                        steps(band, pair)

                band_of_weights(1, 1)
                with dve.Fori(1, BANDS // 2) as pair:
                    for half in range(2):
                        band_of_weights(pair * 2 + half, half)
                reciprocals(BANDS - 1, 1, ROWS, base, 1)

            def general_path():
                row = [P, GROUP, P]
                eye = identf[:, :].unsqueeze(1).to_broadcast(row)
                dve.sem_inc(g_adj_free, 1)
                for k in range(2, RAW_SLOTS):
                    dve.wait_ge(raw_in[k], 16)
                dve.wait_ge(s1_copied, GROUPS + 2)
                link(nc.vector.memset(wt[:, :], 1.0))
                here = links[0]
                with dve.Fori(0, GROUPS) as g:
                    block_of_rbc = rbc[:, bass.ds(g * GROUP * P, GROUP * P)]

                    def chained(k, ins):
                        ins.then_inc(dve_chain, 1)
                        dve.wait_ge(dve_chain, g * 3 + (here + k))

                    chained(1, nc.vector.tensor_tensor(xn[:, 0, :, :], block_of_rbc.rearrange("p (t q) -> p t q", q=P),
                                                       eye, ALU.mult))
                    chained(2, nc.vector.tensor_reduce(s1col[:, bass.ds(g * GROUP, GROUP)], xn[:, 0, :, :],
                                                       AX_X, ALU.add))
                    nc.vector.tensor_tensor(xn[:, 1, :, :],
                                            wh[:, bass.ds(g * GROUP, GROUP), F:FD].to_broadcast(row),
                                            eye, ALU.mult).then_inc(g_diag, 1)
                    dve.wait_ge(g_spread, g + 1)
                    chained(3, nc.vector.tensor_scalar(block_of_rbc.rearrange("p (q b) -> p b q", b=QUAD),
                                                       ps[:, 4, :].rearrange("p (b q) -> p b q", b=QUAD),
                                                       1.0, None, ALU.mult))
                start = here + 3 * GROUPS
                TILE_LINKS = 6

                def tile_of_rows(tile, half):
                    def chained(k, ins):
                        ins.then_inc(dve_chain, 1)
                        dve.wait_ge(dve_chain, tile * TILE_LINKS + (start + k))

                    dve.wait_ge(g_used, tile * (NT // GATHER) + WT_SLOTS)
                    chained(1, nc.vector.tensor_scalar(scores, rbc[:, :], s1col[:, bass.ds(tile, 1)], None, ALU.add))
                    chained(2, nc.vector.scalar_tensor_tensor(scores, scores, SLOPE, scores, ALU.mult, ALU.max))
                    dve.wait_ge(g_adj, tile * 16 + 16)
                    chained(3, nc.vector.scalar_tensor_tensor(scores, adj_rows, 0.0, scores, ALU.is_gt, ALU.mult))
                    chained(4, nc.vector.tensor_scalar(adj_rows.bitcast(F32), adj_rows, 0.0, MASKED,
                                                       ALU.is_le, ALU.mult))
                    chained(5, nc.vector.tensor_tensor(scores, scores, adj_rows.bitcast(F32), ALU.add))
                    dve.sem_inc(g_adj_free, 1)
                    nc.vector.tensor_reduce(nmax[:, :], scores, AX_X, ALU.max, negate=True).then_inc(g_scores, 1)
                    for q in range(NT // GATHER):
                        dve.wait_ge(g_turned, tile * (NT // GATHER) + (q + 1))
                        dve.wait_ge(g_used, tile * (NT // GATHER) + (q + 1))
                        nc.vector.tensor_copy(weights[:, q % WT_SLOTS, :], ps[:, 4 + q % WT_SLOTS, :])\
                            .then_inc(g_copied, 1)
                    reciprocals(tile, half, 1, start + 5, TILE_LINKS)

                with dve.Fori(0, NT // 2) as pair:
                    for half in range(2):
                        tile_of_rows(pair * 2 + half, half)

            with dve.If(safe(dve)):
                safe_path()
                dve.nop()
            with dve.Else():
                general_path()
                dve.nop()
            dve.nop()

        @block.tensor
        def _(pe):
            pe.wait_ge(consts, 3)
            pe.wait_ge(w_in, 16)
            nc.tensor.transpose(ps[:, 4, 0:P], wext[:, 0:F], identf[:, :]).then_inc(wt_turned, 1)
            pe.wait_ge(wt_ready, 1)
            pe.wait_ge(a1_ready, 1)
            nc.tensor.matmul(ps[:, 5, 0:P], wt[:, :], a1bc[:, :], start=True, stop=True)
            nc.tensor.matmul(ps[:, 5, P:P + 1], wt[:, :], a12[:, 1:2], start=True, stop=True).then_inc(wa_done, 1)

            def turn(g, slot):
                pe.wait_ge(xn_ready, g + 1)
                for u in range(GROUP):
                    ins = nc.tensor.transpose(ps[:, 4 + slot, u * P:(u + 1) * P], xn[:, slot, u, :], identf[:, :])
                ins.then_inc(xt_ready, 1)

            def products(g, slot):
                pe.wait_ge(ht_ready, g + 1)
                pe.wait_ge(wh_copied, g + 1)
                for u in range(GROUP):
                    ins = nc.tensor.matmul(acc[slot][:, u // 2, (u % 2) * FD:(u % 2 + 1) * FD],
                                           ht[:, slot, u * P:(u + 1) * P], wext[:, :], start=True, stop=True)
                ins.then_inc(wh_done, 1)
                pe.wait_ge(s1_copied, g + 1)
                nc.tensor.matmul(ps[:, 6 + slot, :], wa1[:, :], ht[:, slot, :], start=True, stop=True)\
                    .then_inc(s1_done, 1)

            pe.wait_ge(wa_ready, 1)
            turn(0, 0)
            with pe.Fori(0, GROUPS // 2 - 1) as pair:
                turn(pair * 2 + 1, 1)
                products(pair * 2, 0)
                turn(pair * 2 + 2, 0)
                products(pair * 2 + 1, 1)
            turn(GROUPS - 1, 1)
            products(GROUPS - 2, 0)
            products(GROUPS - 1, 1)
            pe.wait_ge(hmean_ready, 1)
            nc.tensor.matmul(ps[:, 4, 0:F], hmean[:, :], wext[:, 0:F], start=True, stop=True).then_inc(mwh_done, 1)

            def safe_path():
                pe.wait_ge(mwh_ready, 1)
                pe.wait_ge(wh_copied, GROUPS + 2)
                pe.wait_ge(s1_copied, GROUPS + 2)

                def turn_gates(band, pair, q):
                    slot, inside = q // QUADS % GATE_SLOTS, q % QUADS
                    if inside == 0:
                        pe.wait_ge(gate_ready, band * CHUNKS + pair * 2 + (q // QUADS + 1))
                    for r in range(ROWS):
                        words = gate[:, slot, r, inside * QUAD * P:(inside + 1) * QUAD * P].bitcast(BF16)\
                            .rearrange("p (w c) -> p c w", c=QUAD // PACK)
                        for c in range(QUAD // PACK):
                            ins = nc.tensor.transpose(turned[q % TURNED_SLOTS][:, c, r * P:(r + 1) * P],
                                                      words[:, c, :], identb[:, :])
                    ins.then_inc(turned_ready, 1)

                def multiply(band, pair, u, half, last):
                    pe.wait_ge(weights_ready, band * BAND_STEPS + pair * PAIR + (u + 1))
                    for r in range(ROWS):
                        ins = nc.tensor.matmul(acc[half][:, r // 2, (r % 2) * FD:(r % 2 + 1) * FD],
                                               weights[:, u % WT_SLOTS, r * P:(r + 1) * P],
                                               wh[:, bass.ds(pair * PAIR + u, 1), :].rearrange("p t f -> p (t f)"),
                                               start=False, stop=last and r % 2 == 1, skip_group_check=True)
                    ins.then_inc(weights_used, 1)

                def band_of_products(band, half, last=False):
                    pe.wait_ge(sums_copied, band + 1)
                    for b in range(2):
                        nc.tensor.matmul(acc[half][:, b, :], zeros[:, 0:P], zeros[:, :], start=True, stop=False,
                                         skip_group_check=True)
                    with pe.Fori(0, PAIRS - last) as pair:
                        for u in range(PAIR):
                            if u % QUAD == 0:
                                turn_gates(band, pair, u // QUAD + 1)
                            multiply(band, pair, u, half, False)
                    if last:
                        for u in range(PAIR):
                            if u % QUAD == 0 and u + QUAD < PAIR:
                                turn_gates(band, PAIRS - 1, u // QUAD + 1)
                            multiply(band, PAIRS - 1, u, half, u == PAIR - 1)

                turn_gates(0, 0, 0)
                pe.wait_ge(w_ready, NT // STEPS + 1)
                with pe.Fori(0, BANDS // 2 - 1) as pair:
                    for half in range(2):
                        band_of_products(pair * 2 + half, half)
                band_of_products(BANDS - 2, 0)
                band_of_products(BANDS - 1, 1, last=True)

            def general_path():
                pe.sem_inc(g_used, WT_SLOTS)
                pe.wait_ge(mwh_ready, 1)
                with pe.Fori(0, GROUPS) as g:
                    pe.wait_ge(g_diag, g + 1)
                    nc.tensor.matmul(ps[:, 4, :], wt[:, :], xn[:, 1, :, :].rearrange("p t q -> p (t q)"),
                                     start=True, stop=True).then_inc(g_spread, 1)

                def turn_probs(q):
                    for u in range(GATHER):
                        columns = scores[:, q * QUAD * P:(q + 1) * QUAD * P].rearrange("p (w b) -> p b w", b=QUAD)
                        ins = nc.tensor.transpose(ps[:, 4 + q % WT_SLOTS, u * P:(u + 1) * P],
                                                  columns[:, u, :], identf[:, :])
                    ins.then_inc(g_turned, 1)

                def tile_of_rows(tile, half):
                    pe.wait_ge(g_probs, tile + 1)
                    pe.wait_ge(sums_copied, tile + 1)
                    n = NT // GATHER
                    turn_probs(0)
                    for q in range(n):
                        if q + 1 < n:
                            turn_probs(q + 1)
                        pe.wait_ge(g_copied, tile * n + (q + 1))
                        for u in range(GATHER):
                            ins = nc.tensor.matmul(acc[half][:, 0, 0:F], weights[:, q % WT_SLOTS, u * P:(u + 1) * P],
                                                   wh[:, q * GATHER + u, 0:F],
                                                   start=q + u == 0, stop=q == n - 1 and u == GATHER - 1)
                        ins.then_inc(g_used, 1)

                with pe.Fori(0, NT // 2) as pair:
                    for half in range(2):
                        tile_of_rows(pair * 2 + half, half)

            pe.sem_inc(weights_used, WT_SLOTS)
            with pe.If(safe(pe)):
                safe_path()
                pe.nop()
            with pe.Else():
                general_path()
                pe.nop()
            pe.nop()


_INS = ["x", "adj", "L0_gnn_W", "L0_gnn_a"]
_OUT = ((8192, 128), "float32")


def kernel(**inputs):
    import numpy as _np
    import concourse.bacc as _bacc
    from concourse import mybir as _mybir
    from concourse.bass_utils import run_bass_kernel_spmd as _run

    nc = _bacc.Bacc("TRN2", target_bir_lowering=False, num_devices=1)
    arrays, args = {}, []
    for name in _INS:
        v = _np.ascontiguousarray(inputs[name])
        arrays[f"in_{name}"] = v
        args.append(nc.dram_tensor(f"in_{name}", v.shape, _mybir.dt.from_np(v.dtype), kind="ExternalInput").ap())
    shape, dtype = _OUT
    args.append(nc.dram_tensor("out_x", shape, _mybir.dt.from_np(_np.dtype(dtype)), kind="ExternalOutput").ap())
    graph_attention(nc, *args)
    r = _run(nc, [arrays], core_ids=[0])
    return r.results[0]["out_x"]
```

```python
from contextlib import ExitStack

import concourse.bass as bass
from concourse import mybir

ALU = mybir.AluOpType
ACT = mybir.ActivationFunctionType
AX_X = mybir.AxisListType.X
F32 = mybir.dt.float32
BF16 = mybir.dt.bfloat16
I32 = mybir.dt.int32
U8 = mybir.dt.uint8

P = 128
SLOPE = 0.2
MASKED = -9000000000000000.0
LN_EPS = 1e-5
SAFE_SPREAD = 60.0

QUAD = 4
PACK = 2
ROWS = QUAD
CHUNK = 1024
STEPS = CHUNK // P
RAW_SLOTS = 4
GATE_SLOTS = 2
TURNED_SLOTS = 4
WT_SLOTS = 4
GROUP = QUAD
DVE_TILES = (1, 1, 2, 2)


def graph_attention(nc, x, adj, w, a, out):
    N, F = x.shape
    NT = N // P
    BANDS = N // (ROWS * P)
    BAND = ROWS * P
    CHUNKS = N // CHUNK
    GROUPS = NT // GROUP
    FD = F + 1
    FE = F + 2
    PAIR = 2 * STEPS
    PAIRS = CHUNKS // 2
    BAND_STEPS = NT
    TURN_STEP = STEPS // 2 - 1
    PARTS = 4
    PART = NT // PARTS
    PER_PART = GROUPS // PARTS
    QUADS = CHUNK // (QUAD * P)
    GATHER = QUAD
    assert F == P and CHUNKS % RAW_SLOTS == 0 and QUAD % WT_SLOTS == 0 and BANDS % 2 == 0
    assert len(DVE_TILES) == PER_PART

    with ExitStack() as ctx:
        def sb(name, shape, dt=F32):
            return ctx.enter_context(nc.sbuf_tensor(name, shape, dt))

        def sem(name):
            return ctx.enter_context(nc.semaphore(name))

        raw = sb("raw", [P, RAW_SLOTS, ROWS, CHUNK], I32)
        gate = sb("gate", [P, GATE_SLOTS, ROWS, CHUNK], U8)
        xs = sb("xs", [P, NT, F])
        rbc = sb("rbc", [P, 2, BAND])
        wh = sb("wh", [P, NT, FE])
        s1_band = sb("s1_band", [P, ROWS])
        s2_all = sb("s2_all", [P, N])
        weights = sb("weights", [P, WT_SLOTS, BAND])
        hacc = sb("hacc", [P, 2, ROWS, FD])
        obuf = sb("obuf", [P, 2, ROWS, F])
        hp = sb("hp", [P, ROWS, F])
        neg = sb("neg", [P, ROWS, F])
        xn = weights[:, 0:2, :].rearrange("p s (t f) -> p s t f", f=F)
        ht = weights[:, 2:4, :]
        identf = sb("identf", [P, P])
        identb = sb("identb", [P, P], BF16)
        zeros = sb("zeros", [P, 2 * FD], BF16)
        wext = sb("wext", [P, FE])
        wt = sb("wt", [P, P])
        a21 = sb("a21", [P, 2])
        stats = sb("stats", [P, NT, 6])
        mean = sb("mean", [P, NT])
        rstd = sb("rstd", [P, NT])
        tmp1 = sb("tmp1", [P, NT])
        tmp2 = sb("tmp2", [P, NT])
        hsum = sb("hsum", [P, GROUPS])
        htot = sb("htot", [P, 1])
        hmean = sb("hmean", [P, P])
        mean_wh = sb("mean_wh", [P, F])
        ext = sb("ext", [P, 2])
        gext = sb("gext", [P, 2])
        spread = sb("spread", [P, 1])
        flag = sb("flag", [P, 1], I32)
        bias = sb("bias", [P, 2])
        dcol = sb("dcol", [P, NT])
        beta = sb("beta", [P, NT])
        empty = sb("empty", [P, 2, ROWS])
        rden = sb("rden", [P, 2, ROWS])
        nmax = sb("nmax", [P, 1])

        ps = ctx.enter_context(nc.psum_tensor("ps", [P, 8, 512], F32))
        acc = [ps[:, 2 * k:2 * k + 2, 0:2 * FD] for k in range(2)]
        wh_acc = [ps[:, 2 * k:2 * k + 2, 0:2 * FE] for k in range(2)]
        turned = [ps[:, 4 + k, :].bitcast(BF16).rearrange("p (c i) -> p c i", i=BAND) for k in range(TURNED_SLOTS)]
        turned_bytes = [ps[:, 4 + k, :].bitcast(U8).rearrange("p (c i b) -> p c i b", i=BAND, b=PACK)
                        for k in range(TURNED_SLOTS)]

        w_in, a_in = sem("w_in"), sem("a_in")
        x_in = [sem(f"x_in{k}") for k in range(4)]
        raw_in = [sem(f"raw_in{k}") for k in range(RAW_SLOTS)]
        out_done = [sem(f"out_done{k}") for k in range(2)]
        consts = sem("consts")
        dve_chain, pool_chain, stats_done = sem("dve_chain"), sem("pool_chain"), sem("stats_done")
        wt_turned, wt_ready, wa_done, wa_ready = (
            sem("wt_turned"), sem("wt_ready"), sem("wa_done"), sem("wa_ready"))
        var_ready, std_ready, rstd_ready = sem("var_ready"), sem("std_ready"), sem("rstd_ready")
        xn_ready_pool = sem("xn_ready_pool")
        xn_ready, xt_ready, ht_ready = sem("xn_ready"), sem("xt_ready"), sem("ht_ready")
        wh_done, wh_copied = sem("wh_done"), sem("wh_copied")
        hmean_ready, mwh_done, mwh_ready = sem("hmean_ready"), sem("mwh_done"), sem("mwh_ready")
        ext_ready, gext_ready, flag_ready = sem("ext_ready"), sem("gext_ready"), sem("flag_ready")
        bias_ready = sem("bias_ready")
        s1_ready, s1_turned = sem("s1_ready"), sem("s1_turned")
        d_ready, z_ready, r_ready = sem("d_ready"), sem("z_ready"), sem("r_ready")
        w_first, w_rest = sem("w_first"), sem("w_rest")
        gate_ready = sem("gate_ready")
        turned_ready = sem("turned_ready")
        weights_ready = sem("weights_ready")
        weights_used = sem("weights_used")
        sums_copied = sem("sums_copied")
        hacc_free = sem("hacc_free")
        last_neg, last_exp, last_ready, last_out = (
            sem("last_neg"), sem("last_exp"), sem("last_ready"), sem("last_out"))
        rden_ready, neg_ready, exp_ready, out_ready = (
            sem("rden_ready"), sem("neg_ready"), sem("exp_ready"), sem("out_ready"))
        g_diag, g_spread = sem("g_diag"), sem("g_spread")
        g_adj, g_adj_free = sem("g_adj"), sem("g_adj_free")
        g_scores, g_probs = sem("g_scores"), sem("g_probs")
        g_turned, g_copied, g_used = sem("g_turned"), sem("g_copied"), sem("g_used")

        scores = raw[:, 2:4, :, :].rearrange("p s t j -> p (s t j)").bitcast(F32)
        adj_rows = raw[:, 0:2, :, :].rearrange("p s t j -> p (s t j)")
        x_blocks = x.rearrange("(k p b) f -> p k b f", p=P, b=QUAD)
        adj_blocks = adj.rearrange("(k p b) j -> p k b j", p=P, b=QUAD)
        out_blocks = out.rearrange("(k p b) f -> p k b f", p=P, b=QUAD)

        def safe(eng):
            eng.wait_ge(flag_ready, 1)
            return eng.value_load(flag[0:1, 0:1], min_val=0, max_val=1) == 1

        block = ctx.enter_context(nc.Block())

        @block.sync
        def _(sp):
            sp.dma_start(wext[:, 0:F], w).then_inc(w_in, 16)
            for k in range(2):
                sp.dma_start(a21[:, 1 - k:2 - k], a[k * F:(k + 1) * F, :]).then_inc(a_in, 16)
            for load_of_x, (lo, hi) in enumerate([(0, PART // 2), (PART // 2, PART), (PART, 2 * PART), (2 * PART, NT)]):
                sp.dma_start(xs[:, lo:hi, :].rearrange("p (k b) f -> p k b f", b=QUAD),
                             x_blocks[:, lo // QUAD:hi // QUAD, :, :]).then_inc(x_in[load_of_x], 16)

            def load(band, chunk, slot):
                rows = adj_blocks[:, bass.ds(band, 1), :, chunk * CHUNK:(chunk + 1) * CHUNK]
                sp.dma_start(raw[:, slot, :, :], rows.rearrange("p k b j -> p (k b) j")).then_inc(raw_in[slot], 16)

            for k in range(RAW_SLOTS):
                load(0, k, k)

            def safe_path():
                for k in range(RAW_SLOTS, CHUNKS):
                    sp.wait_ge(gate_ready, k - RAW_SLOTS + 1)
                    load(0, k, k % RAW_SLOTS)
                with sp.Fori(1, BANDS) as band:
                    for k in range(CHUNKS):
                        sp.wait_ge(gate_ready, band * CHUNKS + (k - RAW_SLOTS + 1))
                        load(band, k, k % RAW_SLOTS)
                sp.wait_ge(last_ready, 1)
                sp.dma_start(out_blocks[:, BANDS - 1, :, :],
                             weights[:, 2, :].rearrange("p (b f) -> p b f", f=F)).then_inc(last_out, 16)
                sp.wait_ge(last_out, 16)

            def general_path():
                sp.wait_ge(gate_ready, 1)
                for k in range(RAW_SLOTS):
                    sp.wait_ge(raw_in[k], 16)
                with sp.Fori(0, BANDS) as k:
                    for b in range(QUAD):
                        sp.wait_ge(g_adj_free, k * QUAD + (b + 1))
                        sp.dma_start(adj_rows, adj_blocks[:, bass.ds(k, 1), b, :].rearrange("p k j -> p (k j)"))\
                            .then_inc(g_adj, 16)

            with sp.If(safe(sp)):
                safe_path()
                sp.nop()
            with sp.Else():
                general_path()
                sp.nop()
            sp.nop()

        @block.gpsimd
        def _(pool):
            links = [0]

            def link(ins):
                links[0] += 1
                ins.then_inc(pool_chain, 1)
                pool.wait_ge(pool_chain, links[0])

            pool.sem_inc(hacc_free, 2)
            link(nc.gpsimd.memset(identf[:, :], 0.0))
            link(nc.gpsimd.affine_select(out=identf[:, :], in_=identf[:, :], compare_op=ALU.not_equal, fill=1.0,
                                         base=0, pattern=[[-1, P]], channel_multiplier=1))
            nc.gpsimd.tensor_copy(identb[:, :], identf[:, :]).then_inc(consts, 1)
            nc.gpsimd.memset(zeros[:, :], 0.0).then_inc(consts, 1)
            pool.sem_inc(consts, 1)

            def normalise(k, u, first):
                g = k * PER_PART + u
                if not first:
                    pool.wait_ge(xt_ready, g - 1)
                tiles = GROUP - DVE_TILES[u]
                t = bass.ds(g * GROUP + DVE_TILES[u], tiles)
                row = [P, tiles, F]
                o = xn[:, u % 2, DVE_TILES[u]:GROUP, :]
                nc.gpsimd.tensor_tensor(o, xs[:, t, :], mean[:, t].unsqueeze(2).to_broadcast(row), ALU.subtract)\
                    .then_inc(pool_chain, 1)
                pool.wait_ge(pool_chain, g + (links[0] + 1))
                nc.gpsimd.tensor_tensor(o, o, rstd[:, t].unsqueeze(2).to_broadcast(row), ALU.mult)\
                    .then_inc(xn_ready_pool, 1)

            pool.wait_ge(rstd_ready, 1)
            for u in range(PER_PART):
                normalise(0, u, u < 2)
            with pool.Fori(1, PARTS) as k:
                pool.wait_ge(rstd_ready, k + 1)
                for u in range(PER_PART):
                    normalise(k, u, False)
            links[0] += GROUPS
            pool.wait_ge(ext_ready, 1)
            nc.gpsimd.partition_all_reduce(gext[:, :], ext[:, :], P, bass.bass_isa.ReduceOp.max)\
                .then_inc(gext_ready, 1)

            LINKS = 4
            base = links[0]

            def finish_band(band, half, tiles, first, to, stored=None):
                done = [0]

                def chained(ins):
                    done[0] += 1
                    ins.then_inc(pool_chain, 1)
                    pool.wait_ge(pool_chain, band * LINKS + (base + done[0]))

                h, n, o = hp[:, 0:tiles, :], neg[:, 0:tiles, :], obuf[:, half, 0:tiles, :]
                row = [P, tiles, F]
                pool.wait_ge(rden_ready, band + 1)
                nc.gpsimd.tensor_tensor(n, empty[:, half, 0:tiles].unsqueeze(2).to_broadcast(row),
                                        mean_wh[:, :].unsqueeze(1).to_broadcast(row), ALU.mult)
                chained(nc.gpsimd.tensor_tensor(h, hacc[:, half, 0:tiles, 0:F],
                                                rden[:, half, 0:tiles].unsqueeze(2).to_broadcast(row), ALU.mult))
                chained(nc.gpsimd.tensor_tensor(h, h, n, ALU.add))
                pool.sem_inc(hacc_free, 1)
                nc.gpsimd.tensor_scalar(n, h, 0.0, None, ALU.min).then_inc(neg_ready, 1)
                chained(nc.gpsimd.tensor_scalar(h, h, 0.0, -1.0, ALU.max, ALU.add))
                if stored is not None:
                    pool.wait_ge(out_done[half], stored * 16)
                chained(nc.gpsimd.tensor_tensor(o, h, xs[:, bass.ds(first, tiles), :], ALU.add))
                pool.wait_ge(exp_ready, band + 1)
                nc.gpsimd.tensor_tensor(o, o, n, ALU.add).then_inc(out_ready, 1)
                pool.wait_ge(out_ready, band + 1)
                pool.dma_start(to, o).then_inc(out_done[half], 16)

            def finish_bands():
                def rows(band):
                    return out_blocks[:, bass.ds(band, 1), :, :].rearrange("p k b f -> p (k b) f")

                for half in range(2):
                    finish_band(half, half, ROWS, half * ROWS, rows(half))
                with pool.Fori(1, BANDS // 2 - 1) as pair:
                    for half in range(2):
                        finish_band(pair * 2 + half, half, ROWS, pair * (2 * ROWS) + half * ROWS,
                                    rows(pair * 2 + half), stored=pair)
                finish_band(BANDS - 2, 0, ROWS, (BANDS - 2) * ROWS, rows(BANDS - 2), stored=BANDS // 2 - 1)
                for half in range(2):
                    pool.wait_ge(out_done[half], 16 * (BANDS // 2 - half))

            def finish_tiles():
                for b in range(QUAD):
                    finish_band(b, b % 2, 1, b, out_blocks[:, 0:1, b, :], stored=b // 2 or None)
                with pool.Fori(1, BANDS) as k:
                    for b in range(QUAD):
                        finish_band(k * QUAD + b, b % 2, 1, k * QUAD + b, out_blocks[:, bass.ds(k, 1), b, :],
                                    stored=k * 2 + b // 2)
                for half in range(2):
                    pool.wait_ge(out_done[half], 16 * (NT // 2))

            def safe_path():
                pool.sem_inc(w_rest, 1)
                pool.wait_ge(d_ready, 1)
                with pool.Fori(1, NT // STEPS) as k:
                    part = wh[:, bass.ds(k * STEPS, STEPS), 0:F]
                    d = dcol[:, bass.ds(k * STEPS, STEPS)]
                    nc.gpsimd.tensor_tensor(part, part, d.unsqueeze(2).to_broadcast([P, STEPS, F]), ALU.mult)\
                        .then_inc(w_rest, 1)
                pool.wait_ge(mwh_ready, 1)
                finish_bands()

            with pool.If(safe(pool)):
                safe_path()
                pool.nop()
            with pool.Else():
                pool.wait_ge(mwh_ready, 1)
                finish_tiles()
                pool.nop()
            pool.nop()

        @block.scalar
        def _(act):
            act.sem_inc(sums_copied, 2)
            act.sem_inc(wh_copied, 2)

            def deviations(k):
                act.wait_ge(var_ready, k + 1)
                part = slice(k * PART, (k + 1) * PART)
                nc.scalar.activation(rstd[:, part], tmp2[:, part], ACT.Sqrt).then_inc(std_ready, 1)

            def first_gates(row):
                if row == 0:
                    act.wait_ge(raw_in[0], 16)
                ins = nc.scalar.activation(gate[:, 0, row, :], raw[:, 0, row, :], ACT.Sign)
                if row == ROWS - 1:
                    ins.then_inc(gate_ready, 1)

            def copy_products(g):
                act.wait_ge(wh_done, g + 1)
                nc.scalar.copy(wh[:, g * GROUP:(g + 1) * GROUP, :].rearrange("p (b t) f -> p b (t f)", b=2),
                               wh_acc[g % 2]).then_inc(wh_copied, 1)

            deviations(0)
            for g in range(GROUPS):
                part, u = divmod(g, PER_PART)
                act.wait_ge(xt_ready, g + 1)
                nc.scalar.activation(ht[:, g % 2, :], ps[:, 4 + g % 2, :], ACT.Relu,
                                     accum_out=hsum[:, g:g + 1]).then_inc(ht_ready, 1)
                if u == PER_PART // 2 - 1 and part + 1 < PARTS:
                    deviations(part + 1)
                if g >= 1:
                    copy_products(g - 1)
                if PER_PART < g < PER_PART + 2 * ROWS and g % 2 == 1:
                    first_gates((g - PER_PART) // 2)
            copy_products(GROUPS - 1)
            act.wait_ge(bias_ready, 1)
            nc.scalar.activation(dcol[:, :], wh[:, :, F], ACT.Exp, bias=bias[:, 0:1], scale=SLOPE)\
                .then_inc(d_ready, 1)
            nc.scalar.activation(beta[:, :], wh[:, :, F], ACT.Exp, bias=bias[:, 1:2], scale=1.0 - SLOPE)\
                .then_inc(d_ready, 1)

            def safe_path():
                def form_gates(band, k):
                    act.wait_ge(raw_in[k % RAW_SLOTS], band * (CHUNKS // RAW_SLOTS * 16) + (k // RAW_SLOTS + 1) * 16)
                    if not isinstance(band, int) or band * CHUNKS + k >= GATE_SLOTS:
                        act.wait_ge(turned_ready, band * CHUNKS + (k - GATE_SLOTS + 1))
                    nc.scalar.activation(gate[:, k % GATE_SLOTS, :, :], raw[:, k % RAW_SLOTS, :, :], ACT.Sign).then_inc(gate_ready, 1)

                def copy_sums(band, half):
                    act.wait_ge(weights_used, band * BAND_STEPS + (BAND_STEPS + WT_SLOTS))
                    act.wait_ge(hacc_free, band + 1)
                    nc.scalar.copy(hacc[:, half, :, :].rearrange("p (b t) f -> p b (t f)", b=2), acc[half])\
                        .then_inc(sums_copied, 1)

                def exps(band):
                    act.wait_ge(neg_ready, band + 1)
                    nc.scalar.activation(neg[:, :, :], neg[:, :, :], ACT.Exp).then_inc(exp_ready, 1)

                def exp_rows(band, half):
                    act.wait_ge(z_ready, band + 1)
                    nc.scalar.activation(rbc[:, half, :], rbc[:, half, :], ACT.Exp, scale=SLOPE - 1.0)\
                        .then_inc(r_ready, 1)

                exp_rows(0, 0)
                for k in range(1, CHUNKS):
                    form_gates(0, k)
                exp_rows(1, 1)

                def band_of_gates(band, half, last=False):
                    for k in range(CHUNKS):
                        form_gates(band, k)
                        if k == CHUNKS // 2 - 1:
                            copy_sums(band - 1, 1 - half)
                    if not last:
                        exp_rows(band + 1, 1 - half)
                    exps(band - 1)

                band_of_gates(1, 1)
                with act.Fori(1, BANDS // 2 - 1) as pair:
                    for half in range(2):
                        band_of_gates(pair * 2 + half, half)
                band_of_gates(BANDS - 2, 0)
                band_of_gates(BANDS - 1, 1, last=True)
                act.wait_ge(last_neg, 1)
                nc.scalar.activation(weights[:, 1, :], weights[:, 1, :], ACT.Exp).then_inc(last_exp, 1)

            def general_path():
                def tile_of_rows(tile, half):
                    act.wait_ge(g_scores, tile + 1)
                    act.wait_ge(hacc_free, tile + 1)
                    nc.scalar.activation(scores, scores, ACT.Exp, bias=nmax[:, 0:1],
                                         accum_out=hacc[:, half, 0, F:FD]).then_inc(g_probs, 1)
                    act.wait_ge(g_used, tile * (NT // GATHER) + (NT // GATHER + WT_SLOTS))
                    nc.scalar.copy(hacc[:, half, 0, 0:F], acc[half][:, 0, 0:F]).then_inc(sums_copied, 1)
                    act.wait_ge(neg_ready, tile + 1)
                    nc.scalar.activation(neg[:, 0, :], neg[:, 0, :], ACT.Exp).then_inc(exp_ready, 1)

                with act.Fori(0, NT // 2) as pair:
                    for half in range(2):
                        tile_of_rows(pair * 2 + half, half)

            with act.If(safe(act)):
                safe_path()
                act.nop()
            with act.Else():
                general_path()
                act.nop()
            act.nop()

        @block.vector
        def _(dve):
            links = [0]

            def link(ins):
                links[0] += 1
                ins.then_inc(dve_chain, 1)
                dve.wait_ge(dve_chain, links[0])

            dve.wait_ge(wt_turned, 1)
            nc.vector.tensor_copy(wt[:, :], ps[:, 4, 0:P]).then_inc(wt_ready, 1)

            def statistics(g):
                for u in range(GROUP):
                    t = bass.ds(g * GROUP + u, 1)
                    ins = nc.vector.bn_stats(stats[:, t, :].rearrange("p t s -> p (t s)"),
                                             xs[:, t, :].rearrange("p t s -> p (t s)"))
                ins.then_inc(stats_done, 1)

            def variances(k):
                def chained(n, ins):
                    ins.then_inc(dve_chain, 1)
                    dve.wait_ge(dve_chain, k * 4 + n)

                dve.wait_ge(stats_done, (k + 1) * PER_PART)
                part = bass.ds(k * PART, PART)
                even, odd = stats[:, part, 0:3], stats[:, part, 3:6]
                dif, m, var = tmp1[:, part], mean[:, part], tmp2[:, part]
                nc.vector.tensor_tensor(dif, even[:, :, 1], odd[:, :, 1], ALU.subtract)
                nc.vector.tensor_tensor(m, even[:, :, 1], odd[:, :, 1], ALU.add)
                chained(1, nc.vector.tensor_tensor(var, even[:, :, 2], odd[:, :, 2], ALU.add))
                nc.vector.tensor_scalar(m, m, 0.5, None, ALU.mult)
                chained(2, nc.vector.tensor_tensor(dif, dif, dif, ALU.mult))
                chained(3, nc.vector.scalar_tensor_tensor(var, dif, F / 4, var, ALU.mult, ALU.add))
                nc.vector.tensor_scalar(var, var, 1.0 / F, LN_EPS, ALU.mult, ALU.add).then_inc(var_ready, 1)

            def deviations(k):
                part = bass.ds(k * PART, PART)
                dve.wait_ge(std_ready, k + 1)
                nc.vector.reciprocal(rstd[:, part], rstd[:, part]).then_inc(dve_chain, 1)
                dve.wait_ge(dve_chain, k * 4 + 4)
                dve.sem_inc(rstd_ready, 1)

            def normalise(g, slot, tiles):
                for u in range(tiles):
                    t = g * GROUP + u
                    ins = nc.vector.tensor_scalar(xn[:, slot, u:u + 1, :].rearrange("p t f -> p (t f)"),
                                                  xs[:, bass.ds(t, 1), :].rearrange("p t f -> p (t f)"),
                                                  mean[:, bass.ds(t, 1)], rstd[:, bass.ds(t, 1)],
                                                  ALU.subtract, ALU.mult)
                ins.then_inc(xn_ready, 1)

            for g in range(PER_PART):
                if g % 2 == 0:
                    dve.wait_ge(x_in[g // 2], 16)
                statistics(g)
            variances(0)
            deviations(0)
            dve.wait_ge(wa_done, 1)
            nc.vector.tensor_copy(wext[:, F:FE], ps[:, 5, 0:2]).then_inc(wa_ready, 1)

            def part_of_groups(k, first, last):
                for u in range(PER_PART):
                    if not (first and u < 2):
                        dve.wait_ge(xt_ready, k * PER_PART + (u - 1))
                    normalise(k * PER_PART + u, u % 2, DVE_TILES[u])
                    if u < PER_PART // 2 and not last:
                        if first and u == 0:
                            dve.wait_ge(x_in[2], 16)
                        for v in range(2):
                            statistics((k + 1) * PER_PART + (2 * u + v))
                        if u == PER_PART // 2 - 1:
                            variances(k + 1)
                if not last:
                    deviations(k + 1)

            part_of_groups(0, True, False)
            dve.wait_ge(x_in[3], 16)
            for k in range(1, PARTS):
                part_of_groups(k, False, k == PARTS - 1)
            links[0] = PARTS * 4
            dve.wait_ge(wh_copied, GROUPS + 2)

            def s1_of_band(band):
                nc.vector.tensor_scalar(s1_band[:, :], wh[:, bass.ds(band * ROWS, ROWS), F + 1], 1.0, None, ALU.mult)\
                    .then_inc(s1_ready, 1)

            def z_of_band(band, half):
                dve.wait_ge(s1_turned, band + 1)
                nc.vector.tensor_scalar(rbc[:, half, :], ps[:, 2 * half, :], gext[:, 0:1], 0.0, ALU.add, ALU.max)\
                    .then_inc(z_ready, 1)

            s1_of_band(0)

            nc.vector.tensor_scalar(tmp1[:, :], wh[:, :, F], -1.0, None, ALU.mult)
            link(nc.vector.tensor_reduce(ext[:, 0:1], wh[:, :, F], AX_X, ALU.max))
            nc.vector.tensor_reduce(ext[:, 1:2], tmp1[:, :], AX_X, ALU.max).then_inc(ext_ready, 1)
            dve.wait_ge(ht_ready, GROUPS)
            link(nc.vector.tensor_reduce(htot[:, :], hsum[:, :], AX_X, ALU.add))
            nc.vector.tensor_scalar(hmean[:, :], htot[:, 0:1].to_broadcast([P, P]), 1.0 / N, None, ALU.mult)\
                .then_inc(hmean_ready, 1)
            dve.wait_ge(gext_ready, 1)
            nc.vector.tensor_scalar(bias[:, 0:1], gext[:, 0:1], -SLOPE, None, ALU.mult)
            nc.vector.tensor_scalar(bias[:, 1:2], gext[:, 0:1], SLOPE - 1.0, None, ALU.mult).then_inc(bias_ready, 1)
            link(nc.vector.tensor_tensor(spread[:, :], gext[:, 0:1], gext[:, 1:2], ALU.add))
            nc.vector.tensor_scalar(flag[:, :], spread[:, :], SAFE_SPREAD, None, ALU.is_le).then_inc(flag_ready, 1)
            z_of_band(0, 0)
            dve.wait_ge(mwh_done, 1)
            nc.vector.tensor_copy(mean_wh[:, :], ps[:, 4, 0:F]).then_inc(mwh_ready, 1)

            LINKS = 1
            base = links[0]

            def reciprocals(band, half, tiles, first_link, links_per_band):
                dve.wait_ge(sums_copied, band + 3)
                den = hacc[:, half, 0:tiles, F]
                nc.vector.tensor_scalar(empty[:, half, 0:tiles], den, 0.0, None, ALU.is_le)
                nc.vector.scalar_tensor_tensor(rden[:, half, 0:tiles], den, 0.0, den, ALU.is_le, ALU.add)\
                    .then_inc(dve_chain, 1)
                dve.wait_ge(dve_chain, band * links_per_band + (first_link + 1))
                nc.vector.reciprocal(rden[:, half, 0:tiles], rden[:, half, 0:tiles]).then_inc(rden_ready, 1)

            def safe_path():
                dve.wait_ge(d_ready, 2)
                nc.vector.tensor_tensor(wh[:, 0:STEPS, 0:F], wh[:, 0:STEPS, 0:F],
                                        dcol[:, 0:STEPS].unsqueeze(2).to_broadcast([P, STEPS, F]), ALU.mult)\
                    .then_inc(w_first, 1)
                nc.vector.tensor_copy(wh[:, :, F], dcol[:, :]).then_inc(w_first, 1)

                def steps(band, half, pair):
                    for u in range(PAIR):
                        jt = pair * PAIR + u
                        if u % STEPS == 0:
                            dve.wait_ge(turned_ready, band * CHUNKS + pair * 2 + (u // STEPS + 1))
                        dve.wait_ge(weights_used, band * BAND_STEPS + (jt + 1))
                        nc.vector.scalar_tensor_tensor(
                            weights[:, u % WT_SLOTS, :], rbc[:, half, :],
                            beta[:, bass.ds(jt, 1)], turned_bytes[u // QUAD % TURNED_SLOTS][:, u % QUAD // PACK, :, u % PACK],
                            ALU.max, ALU.min)\
                            .then_inc(weights_ready, 1)

                def last_band(band):
                    links[0] = base + band
                    dve.wait_ge(weights_used, band * BAND_STEPS + (BAND_STEPS + WT_SLOTS))
                    sums = acc[band % 2].rearrange("p b (t f) -> p b t f", f=FD)
                    h, n, o = (weights[:, k, :] for k in range(3))
                    den = sums[:, :, :, F]
                    no_edge = tmp1[:, 0:ROWS].rearrange("p (b t) -> p b t", b=2)
                    r = tmp2[:, 0:ROWS].rearrange("p (b t) -> p b t", b=2)
                    link(nc.vector.tensor_scalar(no_edge, den, 0.0, None, ALU.is_le))
                    link(nc.vector.tensor_tensor(r, den, no_edge, ALU.add))
                    link(nc.vector.reciprocal(r, r))
                    for t in range(ROWS):
                        ins = nc.vector.tensor_scalar(h[:, t * F:(t + 1) * F], sums[:, t // 2, t % 2, 0:F],
                                                      tmp2[:, t:t + 1], None, ALU.mult)
                    link(ins)
                    for t in range(ROWS):
                        columns = slice(t * F, (t + 1) * F)
                        ins = nc.vector.scalar_tensor_tensor(h[:, columns], mean_wh[:, :], tmp1[:, t:t + 1],
                                                             h[:, columns], ALU.mult, ALU.add)
                    link(ins)
                    nc.vector.tensor_scalar(n, h, 0.0, None, ALU.min).then_inc(last_neg, 1)
                    link(nc.vector.scalar_tensor_tensor(
                        o, h, 0.0, xs[:, band * ROWS:(band + 1) * ROWS, :].rearrange("p t f -> p (t f)"),
                        ALU.max, ALU.add))
                    dve.wait_ge(last_exp, 1)
                    nc.vector.scalar_tensor_tensor(o, n, -1.0, o, ALU.add, ALU.add).then_inc(last_ready, 1)

                def band_of_weights(band, half, last=False):
                    dve.wait_ge(r_ready, band + 1)
                    if not last:
                        s1_of_band(band + 1)
                    with dve.Fori(0, PAIRS // 2) as pair:
                        steps(band, half, pair)
                    if not (isinstance(band, int) and band == 0):
                        reciprocals(band - 1, 1 - half, ROWS, base, 1)
                    with dve.Fori(PAIRS // 2, PAIRS - 1) as pair:
                        steps(band, half, pair)
                    if not last:
                        z_of_band(band + 1, 1 - half)
                    steps(band, half, PAIRS - 1)

                band_of_weights(0, 0)
                band_of_weights(1, 1)
                with dve.Fori(1, BANDS // 2 - 1) as pair:
                    for half in range(2):
                        band_of_weights(pair * 2 + half, half)
                band_of_weights(BANDS - 2, 0)
                band_of_weights(BANDS - 1, 1, last=True)
                last_band(BANDS - 1)

            def general_path():
                row = [P, GROUP, P]
                eye = identf[:, :].unsqueeze(1).to_broadcast(row)
                links[0] = base
                dve.sem_inc(g_adj_free, 1)
                for k in range(2, RAW_SLOTS):
                    dve.wait_ge(raw_in[k], 16)
                link(nc.vector.memset(wt[:, :], 1.0))
                here = links[0]
                with dve.Fori(0, GROUPS) as g:
                    nc.vector.tensor_tensor(xn[:, 1, :, :],
                                            wh[:, bass.ds(g * GROUP, GROUP), F:FD].to_broadcast(row),
                                            eye, ALU.mult).then_inc(g_diag, 1)
                    dve.wait_ge(g_spread, g + 1)
                    nc.vector.tensor_scalar(
                        s2_all[:, bass.ds(g * GROUP * P, GROUP * P)].rearrange("p (q b) -> p b q", b=QUAD),
                        ps[:, 4, :].rearrange("p (b q) -> p b q", b=QUAD), 1.0, None, ALU.mult)\
                        .then_inc(dve_chain, 1)
                    dve.wait_ge(dve_chain, g + (here + 1))
                start = here + GROUPS
                TILE_LINKS = 6

                def tile_of_rows(tile, half):
                    def chained(k, ins):
                        ins.then_inc(dve_chain, 1)
                        dve.wait_ge(dve_chain, tile * TILE_LINKS + (start + k))

                    dve.wait_ge(g_used, tile * (NT // GATHER) + WT_SLOTS)
                    chained(1, nc.vector.tensor_scalar(scores, s2_all[:, :], wh[:, bass.ds(tile, 1), F + 1], None, ALU.add))
                    chained(2, nc.vector.scalar_tensor_tensor(scores, scores, SLOPE, scores, ALU.mult, ALU.max))
                    dve.wait_ge(g_adj, tile * 16 + 16)
                    chained(3, nc.vector.scalar_tensor_tensor(scores, adj_rows, 0.0, scores, ALU.is_gt, ALU.mult))
                    chained(4, nc.vector.tensor_scalar(adj_rows.bitcast(F32), adj_rows, 0.0, MASKED,
                                                       ALU.is_le, ALU.mult))
                    chained(5, nc.vector.tensor_tensor(scores, scores, adj_rows.bitcast(F32), ALU.add))
                    dve.sem_inc(g_adj_free, 1)
                    nc.vector.tensor_reduce(nmax[:, :], scores, AX_X, ALU.max, negate=True).then_inc(g_scores, 1)
                    for q in range(NT // GATHER):
                        dve.wait_ge(g_turned, tile * (NT // GATHER) + (q + 1))
                        dve.wait_ge(g_used, tile * (NT // GATHER) + (q + 1))
                        nc.vector.tensor_copy(weights[:, q % WT_SLOTS, :], ps[:, 4 + q % WT_SLOTS, :])\
                            .then_inc(g_copied, 1)
                    reciprocals(tile, half, 1, start + 5, TILE_LINKS)

                with dve.Fori(0, NT // 2) as pair:
                    for half in range(2):
                        tile_of_rows(pair * 2 + half, half)

            with dve.If(safe(dve)):
                safe_path()
                dve.nop()
            with dve.Else():
                general_path()
                dve.nop()
            dve.nop()

        @block.tensor
        def _(pe):
            pe.wait_ge(consts, 3)
            pe.wait_ge(w_in, 16)
            nc.tensor.transpose(ps[:, 4, 0:P], wext[:, 0:F], identf[:, :]).then_inc(wt_turned, 1)
            pe.wait_ge(wt_ready, 1)
            pe.wait_ge(a_in, 32)
            nc.tensor.matmul(ps[:, 5, 0:2], wt[:, :], a21[:, :], start=True, stop=True).then_inc(wa_done, 1)

            def turn(g, slot):
                pe.wait_ge(xn_ready, g + 1)
                pe.wait_ge(xn_ready_pool, g + 1)
                for u in range(GROUP):
                    ins = nc.tensor.transpose(ps[:, 4 + slot, u * P:(u + 1) * P], xn[:, slot, u, :], identf[:, :])
                ins.then_inc(xt_ready, 1)

            def products(g, slot):
                pe.wait_ge(ht_ready, g + 1)
                pe.wait_ge(wh_copied, g + 1)
                for u in range(GROUP):
                    ins = nc.tensor.matmul(wh_acc[slot][:, u // 2, (u % 2) * FE:(u % 2 + 1) * FE],
                                           ht[:, slot, u * P:(u + 1) * P], wext[:, :], start=True, stop=True)
                ins.then_inc(wh_done, 1)

            pe.wait_ge(wa_ready, 1)
            turn(0, 0)
            with pe.Fori(0, GROUPS // 2 - 1) as pair:
                turn(pair * 2 + 1, 1)
                products(pair * 2, 0)
                turn(pair * 2 + 2, 0)
                products(pair * 2 + 1, 1)
            turn(GROUPS - 1, 1)
            products(GROUPS - 2, 0)
            products(GROUPS - 1, 1)
            pe.wait_ge(hmean_ready, 1)
            nc.tensor.matmul(ps[:, 4, 0:F], hmean[:, :], wext[:, 0:F], start=True, stop=True).then_inc(mwh_done, 1)

            def turn_s1(band, half):
                pe.wait_ge(s1_ready, band + 1)
                for r in range(ROWS):
                    ins = nc.tensor.transpose(ps[:, 2 * half, r * P:(r + 1) * P],
                                              s1_band[:, r:r + 1].to_broadcast([P, P]), identf[:, :])
                ins.then_inc(s1_turned, 1)

            turn_s1(0, 0)

            def safe_path():
                pe.wait_ge(mwh_ready, 1)

                def turn_gates(band, pair, k):
                    pe.wait_ge(gate_ready, band * CHUNKS + pair * 2 + (k + 1))
                    for q in range(QUADS):
                        for r in range(ROWS):
                            words = gate[:, k % GATE_SLOTS, r, q * QUAD * P:(q + 1) * QUAD * P].bitcast(BF16)\
                                .rearrange("p (w c) -> p c w", c=QUAD // PACK)
                            for c in range(QUAD // PACK):
                                ins = nc.tensor.transpose(
                                    turned[(k * QUADS + q) % TURNED_SLOTS][:, c, r * P:(r + 1) * P],
                                    words[:, c, :], identb[:, :])
                    ins.then_inc(turned_ready, 1)

                def multiply(band, pair, u, half, last):
                    pe.wait_ge(weights_ready, band * BAND_STEPS + pair * PAIR + (u + 1))
                    if u % STEPS == 0:
                        pe.wait_ge(w_rest, pair * 2 + (u // STEPS + 1))
                    for r in range(ROWS):
                        ins = nc.tensor.matmul(acc[half][:, r // 2, (r % 2) * FD:(r % 2 + 1) * FD],
                                               weights[:, u % WT_SLOTS, r * P:(r + 1) * P],
                                               wh[:, bass.ds(pair * PAIR + u, 1), 0:FD].rearrange("p t f -> p (t f)"),
                                               start=False, stop=last and r % 2 == 1, skip_group_check=True)
                    ins.then_inc(weights_used, 1)

                def band_of_products(band, half, last=False):
                    pe.wait_ge(z_ready, band + 1)
                    for b in range(2):
                        nc.tensor.matmul(acc[half][:, b, :], zeros[:, 0:P], zeros[:, :], start=True, stop=False,
                                         skip_group_check=True)

                    def pair_of_chunks(pair):
                        for u in range(PAIR):
                            if u % STEPS == TURN_STEP:
                                turn_gates(band, pair, u // STEPS + 1)
                            multiply(band, pair, u, half, False)

                    with pe.Fori(0, PAIRS // 2) as pair:
                        pair_of_chunks(pair)
                    if not last:
                        pe.wait_ge(sums_copied, band + 2)
                        turn_s1(band + 1, 1 - half)
                    with pe.Fori(PAIRS // 2, PAIRS - last) as pair:
                        pair_of_chunks(pair)
                    if last:
                        for u in range(PAIR):
                            if u == TURN_STEP:
                                turn_gates(band, PAIRS - 1, 1)
                            multiply(band, PAIRS - 1, u, half, u == PAIR - 1)

                turn_gates(0, 0, 0)
                pe.wait_ge(w_first, 2)
                with pe.Fori(0, BANDS // 2 - 1) as pair:
                    for half in range(2):
                        band_of_products(pair * 2 + half, half)
                band_of_products(BANDS - 2, 0)
                band_of_products(BANDS - 1, 1, last=True)

            def general_path():
                pe.sem_inc(g_used, WT_SLOTS)
                pe.wait_ge(mwh_ready, 1)
                with pe.Fori(0, GROUPS) as g:
                    pe.wait_ge(g_diag, g + 1)
                    nc.tensor.matmul(ps[:, 4, :], wt[:, :], xn[:, 1, :, :].rearrange("p t q -> p (t q)"),
                                     start=True, stop=True).then_inc(g_spread, 1)

                def turn_probs(q):
                    for u in range(GATHER):
                        columns = scores[:, q * QUAD * P:(q + 1) * QUAD * P].rearrange("p (w b) -> p b w", b=QUAD)
                        ins = nc.tensor.transpose(ps[:, 4 + q % WT_SLOTS, u * P:(u + 1) * P],
                                                  columns[:, u, :], identf[:, :])
                    ins.then_inc(g_turned, 1)

                def tile_of_rows(tile, half):
                    pe.wait_ge(g_probs, tile + 1)
                    pe.wait_ge(sums_copied, tile + 1)
                    n = NT // GATHER
                    turn_probs(0)
                    for q in range(n):
                        if q + 1 < n:
                            turn_probs(q + 1)
                        pe.wait_ge(g_copied, tile * n + (q + 1))
                        for u in range(GATHER):
                            ins = nc.tensor.matmul(acc[half][:, 0, 0:F], weights[:, q % WT_SLOTS, u * P:(u + 1) * P],
                                                   wh[:, q * GATHER + u, 0:F],
                                                   start=q + u == 0, stop=q == n - 1 and u == GATHER - 1)
                        ins.then_inc(g_used, 1)

                with pe.Fori(0, NT // 2) as pair:
                    for half in range(2):
                        tile_of_rows(pair * 2 + half, half)

            pe.sem_inc(weights_used, WT_SLOTS)
            with pe.If(safe(pe)):
                safe_path()
                pe.nop()
            with pe.Else():
                general_path()
                pe.nop()
            pe.nop()


_INS = ["x", "adj", "L0_gnn_W", "L0_gnn_a"]
_OUT = ((8192, 128), "float32")


def kernel(**inputs):
    import numpy as _np
    import concourse.bacc as _bacc
    from concourse import mybir as _mybir
    from concourse.bass_utils import run_bass_kernel_spmd as _run

    nc = _bacc.Bacc("TRN2", target_bir_lowering=False, num_devices=1)
    arrays, args = {}, []
    for name in _INS:
        v = _np.ascontiguousarray(inputs[name])
        arrays[f"in_{name}"] = v
        args.append(nc.dram_tensor(f"in_{name}", v.shape, _mybir.dt.from_np(v.dtype), kind="ExternalInput").ap())
    shape, dtype = _OUT
    args.append(nc.dram_tensor("out_x", shape, _mybir.dt.from_np(_np.dtype(dtype)), kind="ExternalOutput").ap())
    graph_attention(nc, *args)
    r = _run(nc, [arrays], core_ids=[0])
    return r.results[0]["out_x"]
```
